# Optimizing a Trainium2 kernel written in Bass

```python
import numpy as np
import jax
import jax.numpy as jnp

def _softmax(x, axis=-1):
    return jax.nn.softmax(x, axis=axis)

def _gelu(x):
    return jax.nn.gelu(x, approximate=True)

def _silu(x):
    return jax.nn.silu(x)

def _sigmoid(x):
    return jax.nn.sigmoid(x)

def _layernorm(x, axis=-1, eps=1e-05):
    m = jnp.mean(x, axis=axis, keepdims=True)
    v = jnp.var(x, axis=axis, keepdims=True)
    return (x - m) / jnp.sqrt(v + eps)

def _scatter_add(tgt, idx, src, axis=0):
    return tgt.at[idx].add(src)

def _segment_sum(src, seg, n):
    return jax.ops.segment_sum(src, seg, n)
kernel_name = 'mk_xattn_ffn_d1_seqx_r4_dfd509'

def setup_inputs(seed: int=0):
    np.random.seed(seed)
    _w = jnp.asarray

    def _rec_inputs():
        import jax
        import jax.numpy as jnp
        _rk = jax.random.key(seed)
        x = -7.109e-05 + 0.9999 * jax.random.normal(jax.random.fold_in(_rk, 1), (8, 256, 1024), jnp.float32)
        _lenS = 256 - jax.random.randint(jax.random.fold_in(_rk, 7), (8,), 0, max(1, 256 // 4) + 1, jnp.int32)
        _lenS2 = 256 - jax.random.randint(jax.random.fold_in(_rk, 8), (8,), 0, max(1, 256 // 4) + 1, jnp.int32)
        _ctx_4096P = jax.random.normal(jax.random.fold_in(_rk, 11), (8, 16, 1024), jnp.float32)
        _ctx_4096c = jax.random.dirichlet(jax.random.fold_in(_rk, 511), 0.3 * jnp.ones((16,), jnp.float32), (8, 256))
        _ctx_4096t = jnp.einsum('bsk,bkd->bsd', _ctx_4096c, _ctx_4096P)
        _ctx_4096t = _ctx_4096t * jax.lax.rsqrt(jnp.mean(jnp.square(_ctx_4096t)) + 1e-12) * 0.953939
        ctx_4096 = -2.6191e-05 + 0.999952 * (_ctx_4096t + 0.3 * jax.random.normal(jax.random.fold_in(_rk, 611), (8, 256, 1024), jnp.float32))
        return (x, ctx_4096)
    x, ctx_4096 = _rec_inputs()

    def _L0_xattn_setup():
        import jax, jax.numpy as jnp
        import numpy as np
        TEXT_DIM = 1024
        FEATURE_DIM = 1024

        def _xavier_uniform(key, shape):
            fan_in, fan_out = (shape[1], shape[0])
            limit = float(np.sqrt(6.0 / (fan_in + fan_out)))
            return jax.random.uniform(key, shape, jnp.float32, -limit, limit)
        key = jax.random.key(seed)
        k1, k2, k3, k4 = jax.random.split(key, 4)
        text = jax.random.normal(k1, (8, 512, TEXT_DIM), jnp.float32)
        features = jax.random.normal(k2, (8, 144, FEATURE_DIM), jnp.float32)
        Wq = _xavier_uniform(k3, (FEATURE_DIM, TEXT_DIM))
        bq = jnp.zeros((FEATURE_DIM,), jnp.float32)
        Wk = _xavier_uniform(k4, (FEATURE_DIM, FEATURE_DIM))
        bk = jnp.zeros((FEATURE_DIM,), jnp.float32)
        return {'text': text, 'features': features, 'Wq': Wq, 'bq': bq, 'Wk': Wk, 'bk': bk}
    _L0_xattn_all = _L0_xattn_setup()
    _L0_xattn_in = {k: v for k, v in _L0_xattn_all.items() if k in ('Wq', 'bq', 'Wk', 'bk')}
    del _L0_xattn_all

    def _L0_ffn_setup():
        import jax, jax.numpy as jnp
        import numpy as np
        BLOCK = 64
        NF4_CODE = jnp.array([-1.0, -0.6961928009986877, -0.5250730514526367, -0.39491748809814453, -0.28444138169288635, -0.18477343022823334, -0.09105003625154495, 0.0, 0.07958029955625534, 0.16093020141124725, 0.24611230194568634, 0.33791524171829224, 0.44070982933044434, 0.5626170039176941, 0.7229568362236023, 1.0], dtype=jnp.float32)

        def dequant_nf4(q, absmax, shape):
            w = NF4_CODE[q.reshape(-1)]
            w = w.reshape(-1, BLOCK) * absmax[:, None]
            return w.reshape(shape)
        key = jax.random.key(seed)
        ks = jax.random.split(key, 7)
        HD, M = (1024, 3584)
        nblk = HD * M // BLOCK
        x = jax.random.normal(ks[0], (2, 512, HD), dtype=jnp.float32)
        gate_q = jax.random.randint(ks[1], (M, HD), 0, 16, dtype=jnp.int32)
        up_q = jax.random.randint(ks[2], (M, HD), 0, 16, dtype=jnp.int32)
        down_q = jax.random.randint(ks[3], (HD, M), 0, 16, dtype=jnp.int32)
        gate_absmax = jax.random.uniform(ks[4], (nblk,), dtype=jnp.float32) * 0.05
        up_absmax = jax.random.uniform(ks[5], (nblk,), dtype=jnp.float32) * 0.05
        down_absmax = jax.random.uniform(ks[6], (nblk,), dtype=jnp.float32) * 0.05
        return {'x': x, 'gate_q': gate_q, 'gate_absmax': gate_absmax, 'up_q': up_q, 'up_absmax': up_absmax, 'down_q': down_q, 'down_absmax': down_absmax}
    _L0_ffn_all = _L0_ffn_setup()
    _L0_ffn_in = {k: v for k, v in _L0_ffn_all.items() if k in ('gate_q', 'gate_absmax', 'up_q', 'up_absmax', 'down_q', 'down_absmax')}
    del _L0_ffn_all
    return {'x': x, 'ctx_4096': ctx_4096, 'L0_xattn_Wq': _L0_xattn_in['Wq'], 'L0_xattn_bq': _L0_xattn_in['bq'], 'L0_xattn_Wk': _L0_xattn_in['Wk'], 'L0_xattn_bk': _L0_xattn_in['bk'], 'L0_ffn_gate_q': _L0_ffn_in['gate_q'], 'L0_ffn_gate_absmax': _L0_ffn_in['gate_absmax'], 'L0_ffn_up_q': _L0_ffn_in['up_q'], 'L0_ffn_up_absmax': _L0_ffn_in['up_absmax'], 'L0_ffn_down_q': _L0_ffn_in['down_q'], 'L0_ffn_down_absmax': _L0_ffn_in['down_absmax']}

def reference(x, ctx_4096, L0_xattn_Wq, L0_xattn_bq, L0_xattn_Wk, L0_xattn_bk, L0_ffn_gate_q, L0_ffn_gate_absmax, L0_ffn_up_q, L0_ffn_up_absmax, L0_ffn_down_q, L0_ffn_down_absmax):
    import jax
    import jax.numpy as jnp

    def _L0_xattn_ref(text, features, Wq, bq, Wk, bk):
        import jax, jax.numpy as jnp
        import numpy as np
        TEXT_DIM = 1024
        FEATURE_DIM = 1024

        def _xavier_uniform(key, shape):
            fan_in, fan_out = (shape[1], shape[0])
            limit = float(np.sqrt(6.0 / (fan_in + fan_out)))
            return jax.random.uniform(key, shape, jnp.float32, -limit, limit)
        Q = jnp.einsum('btx,dx->btd', text, Wq) + bq
        K = jnp.einsum('bpx,dx->bpd', features, Wk) + bk
        scale = 1.0 / jnp.sqrt(jnp.asarray(K.shape[-1], K.dtype))
        scores = jnp.einsum('btd,bpd->btp', Q, K) * scale
        attn = jax.nn.softmax(scores, axis=-1)
        attended = jnp.einsum('btp,bpd->btd', attn, features)
        return attended

    def _L0_ffn_ref(x, gate_q, gate_absmax, up_q, up_absmax, down_q, down_absmax):
        import jax, jax.numpy as jnp
        import numpy as np
        BLOCK = 64
        NF4_CODE = jnp.array([-1.0, -0.6961928009986877, -0.5250730514526367, -0.39491748809814453, -0.28444138169288635, -0.18477343022823334, -0.09105003625154495, 0.0, 0.07958029955625534, 0.16093020141124725, 0.24611230194568634, 0.33791524171829224, 0.44070982933044434, 0.5626170039176941, 0.7229568362236023, 1.0], dtype=jnp.float32)

        def dequant_nf4(q, absmax, shape):
            w = NF4_CODE[q.reshape(-1)]
            w = w.reshape(-1, BLOCK) * absmax[:, None]
            return w.reshape(shape)
        HD = x.shape[-1]
        M = gate_q.shape[0]
        Wg = dequant_nf4(gate_q, gate_absmax, (M, HD))
        Wu = dequant_nf4(up_q, up_absmax, (M, HD))
        Wd = dequant_nf4(down_q, down_absmax, (HD, M))
        g = jnp.einsum('bsh,mh->bsm', x, Wg)
        u = jnp.einsum('bsh,mh->bsm', x, Wu)
        h = jax.nn.silu(g) * u
        return jnp.einsum('bsm,hm->bsh', h, Wd)
    x = x + _L0_xattn_ref(_layernorm(x, axis=-1), ctx_4096, L0_xattn_Wq, L0_xattn_bq, L0_xattn_Wk, L0_xattn_bk)
    x = x + _L0_ffn_ref(_layernorm(x, axis=-1), L0_ffn_gate_q, L0_ffn_gate_absmax, L0_ffn_up_q, L0_ffn_up_absmax, L0_ffn_down_q, L0_ffn_down_absmax)
    return x

_drawn_inputs = setup_inputs


def setup_inputs(seed=0):
    import zlib

    import numpy as np

    out = dict(_drawn_inputs(seed))
    spreads = {'L0_xattn_bq': (0.0, 0.423), 'L0_xattn_bk': (0.0, 0.8)}
    factors = {}
    for name, (base, spread) in spreads.items():
        noise = np.random.default_rng([zlib.crc32(name.encode()), seed]).standard_normal(out[name].shape)
        drawn = base * np.exp(spread * noise) if base else spread * noise
        out[name] = jnp.asarray(drawn.astype(out[name].dtype))
    for name, factor in factors.items():
        out[name] = (out[name] * factor).astype(out[name].dtype)
    return out
```

```python
from contextlib import ExitStack

import numpy as np

import concourse.bass as bass
from concourse import mybir

ALU = mybir.AluOpType
ACT = mybir.ActivationFunctionType
AX = mybir.AxisListType
F32 = mybir.dt.float32
F16 = mybir.dt.float16
I32 = mybir.dt.int32

P = 128
BANK = 512
BATCH, SEQ, DIM = 8, 256, 1024
HID = 3584
QBLOCK = 64
TOK = BATCH * SEQ
KT = DIM // P
NT = TOK // P
TB = SEQ // P
CH = HID // P
KB = DIM // QBLOCK
MB = HID // QBLOCK
EPS = 1e-5
SCORE_SCALE = float(DIM) ** -0.5

X_SCALE = 1024.0
W_SCALE = 1024.0
H_BOUND_SCALE = 2.0 ** -5
TINY = 1e-15

ZERO_CODE = 7.0
FACTORS = [
    (0.16843146085739136, -2.5078866481781006, 0.005980083718895912),
    (0.16843146085739136, -1.8140839338302612, 0.1702844202518463),
    (0.16843146085739136, -2.2222657203674316, 0.07722912728786469),
    (0.16843144595623016, -0.31645941734313965, 0.07142763584852219),
    (0.16843146085739136, -0.7382349967956543, 0.15366360545158386),
    (0.16843147575855255, -1.310221791267395, 0.17072737216949463),
    (0.16843146085739136, -0.024128910154104233, 0.005195258650928736),
]
NF = len(FACTORS)

GU_EVENT = {0: (0, 0), 1: (0, 1), 2: (0, 2), 3: (0, 3), 8: (1, 0), 9: (1, 1), 10: (1, 2), 11: (1, 3)}
DOWN_EVENT = {4: 0, 5: 1, 6: 2, 7: 3}
EVENTS = 12
PERIODS = CH // 2
FIRST_UNITS = 4
UNITS = 6 * CH
LEAD = 2
NBLK = TOK // BANK
Q_RING, P_RING = 3, 3


def unit_of(p, e):
    u = FIRST_UNITS + EVENTS * p + e
    if e < 4:
        return u, 2 * p + 1, (e // 2, e % 2)
    if e < 6:
        return u, 2 * p, (2, e - 4)
    if e < 10:
        return u, 2 * p + 2, ((e - 6) // 2, e % 2)
    return u, 2 * p + 1, (2, e - 10)


def has_unit(p, e):
    return not (isinstance(p, int) and p == PERIODS - 1 and 6 <= e < 10)


def slot_of(odd, parity):
    return 1 if odd else 2 * parity


def wait(eng, sem, count):
    if not isinstance(count, int) or count > 0:
        eng.wait_ge(sem, count)


def xattn_ffn_kernel(nc, x, ctx, Wq, bq, Wk, bk, gate_q, gate_absmax, up_q, up_absmax, down_q, down_absmax, out):
    x_t = x.rearrange("b (t p) d -> p (b t) d", p=P)
    out_t = out.rearrange("b (t p) d -> p (b t) d", p=P)
    with ExitStack() as whole:
        def sb(name, shape, dt, stack=whole):
            return stack.enter_context(nc.sbuf_tensor(name, shape, dt))

        y = sb("y", [P, NT, DIM], F32)
        ident = sb("ident", [P, P], F32)
        sg = sb("sg", [P, CH, KB], F32)
        su = sb("su", [P, CH, KB], F32)
        sd = sb("sd", [P, KT, MB], F32)
        gate_out = sb("gate_out", [P, CH], F32)
        up_out = sb("up_out", [P, CH], F32)
        y_out = sb("y_out", [P, 1], F32)
        mv = sb("mv", [P, NT, 2], F32)
        rstd = sb("rstd", [P, NT], F32)
        ps = whole.enter_context(nc.psum_tensor("ps", [P, 8, BANK], F32))

        with ExitStack() as attn:
            A = sb("A", [P, KT, DIM], F32, attn)
            small = sb("small", [P, 17], F32, attn)
            with ExitStack() as st:
                prepare(nc, st, locals())
            with ExitStack() as st:
                attend(nc, st, locals())
        with ExitStack() as st:
            feed_forward(nc, st, locals())


def prepare(nc, st, t):
    y, ident, sg, su, sd, A, small, ps, mv, rstd = (t[n] for n in ("y", "ident", "sg", "su", "sd", "A", "small", "ps", "mv", "rstd"))
    gate_out, up_out, y_out, x_t = t["gate_out"], t["up_out"], t["y_out"], t["x_t"]

    def sb(name, shape, dt):
        return st.enter_context(nc.sbuf_tensor(name, shape, dt))

    def sem(name):
        return st.enter_context(nc.semaphore(name))

    XQ = 4
    wq = sb("wq", [P, KT, DIM], F32)
    wk = sb("wk", [P, KT, DIM], F32)
    bqk = sb("bqk", [P, 2, KT], F32)
    prod = sb("prod", [P, KT], F32)
    bsum = sb("bsum", [P, 1], F32)
    ones = sb("ones", [P, P], F32)
    stats = sb("stats", [P, NT, 2, 6], F32)
    std = sb("std", [P, NT], F32)
    Sg = sb("Sg", [P, CH], F32)
    Su = sb("Su", [P, CH], F32)
    Rg = sb("Rg", [P, CH], F32)
    Ru = sb("Ru", [P, CH], F32)
    SS = sb("SS", [P, CH], F32)
    top = sb("top", [P, 2], F32)
    topall = sb("topall", [P, 2], F32)
    rtop = sb("rtop", [P, 2], F32)
    s_w = [sem(f"s_w{k}") for k in range(KT)]
    s_x = [sem(f"s_x{k}") for k in range(XQ)]
    s_b, s_abs, s_id, s_prod = sem("s_b"), sem("s_abs"), sem("s_id"), sem("s_prod")
    s_acc, s_ev0, s_ev1, s_small = sem("s_acc"), sem("s_ev0"), sem("s_ev1"), sem("s_small")
    s_small_ev, s_top, s_topall, s_var, s_std, s_self = (sem("s_small_ev"), sem("s_top"), sem("s_topall"),
                                                        sem("s_var"), sem("s_std"), sem("s_self"))
    HALVES = DIM // BANK

    with nc.Block() as block:
        @block.sync
        def _(sp):
            for k in range(KT):
                sp.dma_start(wq[:, k, :], t["Wq"][k * P:(k + 1) * P, :]).then_inc(s_w[k], 16)
                sp.dma_start(wk[:, k, :], t["Wk"][k * P:(k + 1) * P, :]).then_inc(s_w[k], 16)

        @block.scalar
        def _(act):
            act.dma_start(bqk[:, 0, :], t["bq"].rearrange("(k p) -> p k", p=P),
                          allow_slow_non_contiguous=True).then_inc(s_b, 16)
            act.dma_start(bqk[:, 1, :], t["bk"].rearrange("(k p) -> p k", p=P),
                          allow_slow_non_contiguous=True).then_inc(s_b, 16)
            act.dma_start(sg[:, :, :], t["gate_absmax"].rearrange("(c p b) -> p c b", p=P, b=KB)).then_inc(s_abs, 16)
            act.dma_start(su[:, :, :], t["up_absmax"].rearrange("(c p b) -> p c b", p=P, b=KB)).then_inc(s_abs, 16)
            act.dma_start(sd[:, :, :], t["down_absmax"].rearrange("(k p b) -> p k b", p=P, b=MB)).then_inc(s_abs, 16)
            for n in range(XQ):
                tiles = slice(n * NT // XQ, (n + 1) * NT // XQ)
                act.dma_start(y[:, tiles, :], x_t[:, tiles, :]).then_inc(s_x[n], 16)
            for h in range(HALVES):
                for i in range(1, KT, 2):
                    act.wait_ge(s_acc, h * KT + i + 1)
                    nc.scalar.copy(A[:, i, h * BANK:(h + 1) * BANK], ps[:, i, :]).then_inc(s_ev1, 1)
            act.wait_ge(s_var, 1)
            nc.scalar.activation(std[:, :], rstd[:, :], ACT.Sqrt).then_inc(s_std, 1)

        @block.gpsimd
        def _(pool):
            nc.gpsimd.memset(ident[:, :], 0.0).then_inc(s_id, 1)
            nc.gpsimd.memset(ones[:, :], 1.0).then_inc(s_id, 1)
            pool.wait_ge(s_id, 2)
            nc.gpsimd.affine_select(out=ident[:, :], in_=ident[:, :], compare_op=ALU.not_equal, fill=1.0, base=0,
                                    pattern=[[-1, P]], channel_multiplier=1).then_inc(s_id, 1)
            pool.wait_ge(s_top, 1)
            nc.gpsimd.partition_all_reduce(topall[:, :], top[:, :], P, bass.bass_isa.ReduceOp.max).then_inc(s_topall, 1)

        @block.tensor
        def _(pe):
            for h in range(HALVES):
                for k in range(KT):
                    if h == 0:
                        pe.wait_ge(s_w[k], 32)
                    for i in range(KT):
                        if h and k == 0:
                            pe.wait_ge((s_ev0, s_ev1)[i % 2], (h - 1) * KT // 2 + i // 2 + 1)
                        last = nc.tensor.matmul(ps[:, i, :], wq[:, k, i * P:(i + 1) * P], wk[:, k, h * BANK:(h + 1) * BANK],
                                                start=k == 0, stop=k == KT - 1)
                        if k == KT - 1:
                            last.then_inc(s_acc, 1)
            pe.wait_ge(s_ev0, HALVES * KT // 2)
            pe.wait_ge(s_b, 32)
            pe.wait_ge(s_id, 3)
            pe.wait_ge(s_prod, 1)
            for col, (w, b) in enumerate(((wk, 0), (wq, 1))):
                for i in range(KT):
                    n = col * KT + i
                    for k in range(KT):
                        nc.tensor.matmul(ps[:, 0, n:n + 1], w[:, k, i * P:(i + 1) * P], bqk[:, b, k:k + 1],
                                         start=k == 0, stop=k == KT - 1)
            nc.tensor.matmul(ps[:, 0, 16:17], ones[:, :], bsum[:, :], start=True, stop=True).then_inc(s_small, 1)

        @block.vector
        def _(dve):
            done = [0]

            def link(op):
                done[0] += 1
                op.then_inc(s_self, 1)
                dve.wait_ge(s_self, done[0])

            dve.wait_ge(s_b, 32)
            link(nc.vector.tensor_tensor(prod[:, :], bqk[:, 0, :], bqk[:, 1, :], ALU.mult))
            nc.vector.reduce_sum(bsum[:, :], prod[:, :], axis=AX.X).then_inc(s_prod, 1)
            dve.wait_ge(s_abs, 48)
            for S, s in ((Sg, sg), (Su, su)):
                link(nc.vector.tensor_reduce(S[:, :], s[:, :, :], axis=AX.X, op=ALU.max, apply_absolute_value=True))
                link(nc.vector.tensor_scalar(S[:, :], S[:, :], TINY, None, ALU.max))
            link(nc.vector.tensor_tensor(SS[:, :], Sg[:, :], Su[:, :], ALU.mult))
            link(nc.vector.tensor_reduce(top[:, 0:1], SS[:, :], axis=AX.X, op=ALU.max))
            link(nc.vector.tensor_reduce(top[:, 1:2], sd[:, :, :], axis=AX.XY, op=ALU.max, apply_absolute_value=True))
            nc.vector.tensor_scalar(top[:, 1:2], top[:, 1:2], TINY, None, ALU.max).then_inc(s_top, 1)
            for S, R, s in ((Sg, Rg, sg), (Su, Ru, su)):
                link(nc.vector.reciprocal(R[:, :], S[:, :]))
                link(nc.vector.tensor_scalar(R[:, :], R[:, :], W_SCALE, None, ALU.mult))
                nc.vector.tensor_tensor(s[:, :, :], s[:, :, :],
                                        R[:, :].rearrange("p (c o) -> p c o", o=1).broadcast_to([P, CH, KB]), ALU.mult)
            nc.vector.tensor_scalar(gate_out[:, :], Sg[:, :], 1.0 / (X_SCALE * W_SCALE), None, ALU.mult)
            dve.wait_ge(s_topall, 1)
            link(nc.vector.reciprocal(rtop[:, :], topall[:, :]))
            nc.vector.tensor_scalar(up_out[:, :], Su[:, :], rtop[:, 0:1], H_BOUND_SCALE / (X_SCALE * W_SCALE), ALU.mult, ALU.mult)
            nc.vector.tensor_scalar(sd[:, :, :], sd[:, :, :], rtop[:, 1:2], W_SCALE, ALU.mult, ALU.mult)
            nc.vector.tensor_scalar(y_out[:, :], topall[:, 0:1], topall[:, 1:2], 1.0 / (H_BOUND_SCALE * W_SCALE),
                                    ALU.mult, ALU.mult)
            for n in range(XQ):
                dve.wait_ge(s_x[n], 16)
                for i in range(n * NT // XQ, (n + 1) * NT // XQ):
                    nc.vector.bn_stats(stats[:, i, 0, :], y[:, i, 0:BANK])
                    link(nc.vector.bn_stats(stats[:, i, 1, :], y[:, i, BANK:DIM]))
                    last = nc.vector.bn_aggr(mv[:, i, :], stats[:, i, :, :].rearrange("p a b -> p (a b)"))
                if n == 1:
                    for i in range(0, KT, 2):
                        dve.wait_ge(s_acc, i + 1)
                        nc.vector.tensor_copy(A[:, i, 0:BANK], ps[:, i, :]).then_inc(s_ev0, 1)
            link(last)
            nc.vector.tensor_scalar(rstd[:, :], mv[:, :, 1], EPS, None, ALU.add).then_inc(s_var, 1)
            for i in range(0, KT, 2):
                dve.wait_ge(s_acc, KT + i + 1)
                nc.vector.tensor_copy(A[:, i, BANK:DIM], ps[:, i, :]).then_inc(s_ev0, 1)
            dve.wait_ge(s_std, 1)
            nc.vector.reciprocal(rstd[:, :], std[:, :])
            dve.wait_ge(s_small, 1)
            nc.vector.tensor_copy(small[:, :], ps[:, 0, 0:17]).then_inc(s_small_ev, 1)


def attend(nc, st, t):
    y, ident, A, small, ps, mv, rstd = (t[n] for n in ("y", "ident", "A", "small", "ps", "mv", "rstd"))
    ctx_dram = t["ctx"].rearrange("b (t p) d -> b p t d", p=P)

    def sb(name, shape, dt):
        return st.enter_context(nc.sbuf_tensor(name, shape, dt))

    def sem(name):
        return st.enter_context(nc.semaphore(name))

    keys = sb("keys", [P, 2, TB, DIM], F32)
    keysT = sb("keysT", [P, KT, SEQ], F32)
    xn = sb("xn", [P, TB, DIM], F32)
    xnT = sb("xnT", [P, KT, SEQ], F32)
    RT = sb("RT", [P, KT, SEQ], F32)
    probs = sb("probs", [P, TB, SEQ], F32)
    probsT = sb("probsT", [P, TB, SEQ], F32)
    sums = sb("sums", [P, TB], F32)
    rsum = sb("rsum", [P, 2, TB], F32)
    mx = sb("mx", [P, TB], F32)
    row = sb("row", [P, TB], F32)
    top = sb("top_s", [P, TB], F32)
    dif = sb("dif", [P, TB], F32)
    neg = sb("neg", [P, TB], F32)
    s_keys = [sem("s_keys0"), sem("s_keys1")]
    s_xn, s_t, s_tev, s_r, s_rev, s_scores, s_neg, s_probs = (
        sem(n) for n in ("s_xn", "s_t", "s_tev", "s_r", "s_rev", "s_scores", "s_neg", "s_probs"))
    s_pt, s_ptev, s_att, s_y, s_self = (sem(n) for n in ("s_pt", "s_ptev", "s_att", "s_y", "s_selfb"))
    TG = 2 * 2 * TB
    HALVES = DIM // BANK
    ATT = TB * HALVES

    def stage(eng_loop, step):
        step(0, 0)
        with eng_loop(0, (BATCH - 2) // 2) as j:
            step(2 * j + 1, 1)
            step(2 * j + 2, 0)
        step(BATCH - 1, 1)

    with nc.Block() as block:
        @block.sync
        def _(sp):
            def load(b, parity):
                if not isinstance(b, int) or b >= 2:
                    sp.wait_ge(s_att, ATT * (b - 1))
                sp.dma_start(keys[:, parity, :, :],
                             ctx_dram[bass.ds(b, 1)].rearrange("o p t d -> p (o t) d")).then_inc(s_keys[parity], 16)

            load(0, 0)
            load(1, 1)
            with nc.sync.Fori(0, (BATCH - 2) // 2) as j:
                load(2 * j + 2, 0)
                load(2 * j + 3, 1)

        @block.tensor
        def _(pe):
            def turn(b, g, src):
                wait(pe, s_tev, TG * b + g - 1)
                for k in range(4):
                    last = nc.tensor.transpose(ps[:, g % 2, k * P:(k + 1) * P], src[:, k * P:(k + 1) * P], ident[:, :])
                last.then_inc(s_t, 1)

            def finish(b, parity):
                pe.wait_ge(s_ptev, b + 1)
                for i in range(TB):
                    for h in range(HALVES):
                        n = i * HALVES + h
                        if n >= 2:
                            pe.wait_ge(s_y, ATT * b + n - 1)
                        for k in range(TB):
                            last = nc.tensor.matmul(ps[:, 6 + n % 2, :], probsT[:, k, i * P:(i + 1) * P],
                                                    keys[:, parity, k, h * BANK:(h + 1) * BANK],
                                                    start=k == 0, stop=k == TB - 1)
                        last.then_inc(s_att, 1)

            def turn_probs(b):
                pe.wait_ge(s_probs, TB * (b + 1))
                for k in range(TB):
                    for i in range(TB):
                        last = nc.tensor.transpose(ps[:, 4, (k * TB + i) * P:(k * TB + i + 1) * P],
                                                   probs[:, i, k * P:(k + 1) * P], ident[:, :])
                last.then_inc(s_pt, 1)

            def step(b, parity):
                first = isinstance(b, int) and b == 0
                for i in range(TB):
                    pe.wait_ge(s_xn, TB * b + i + 1)
                    for h in range(HALVES):
                        turn(b, i * HALVES + h, xn[:, i, h * BANK:(h + 1) * BANK])
                pe.wait_ge(s_keys[parity], 16 * (b // 2 + 1) if isinstance(b, int) else 8 * (b + 2 - parity))
                for i in range(TB):
                    for h in range(HALVES):
                        turn(b, TB * HALVES + i * HALVES + h, keys[:, parity, i, h * BANK:(h + 1) * BANK])
                pe.wait_ge(s_tev, TG * b + TB * HALVES)
                for o in range(KT):
                    wait(pe, s_rev, KT * b + o - 1)
                    for k in range(KT):
                        last = nc.tensor.matmul(ps[:, 2 + o % 2, 0:SEQ], A[:, k, o * P:(o + 1) * P], xnT[:, k, :],
                                                start=k == 0, stop=k == KT - 1)
                    last.then_inc(s_r, 1)
                    if o == KT // 2 - 1 and not first:
                        turn_probs(b - 1)
                if not first:
                    finish(b - 1, 1 - parity)
                pe.wait_ge(s_rev, KT * (b + 1))
                pe.wait_ge(s_tev, TG * (b + 1))
                for i in range(TB):
                    for k in range(KT):
                        nc.tensor.matmul(ps[:, 4 + i, SEQ:SEQ + 1], xnT[:, k, i * P:(i + 1) * P],
                                         small[:, KT + k:KT + k + 1], start=k == 0, stop=k == KT - 1)
                    for k in range(KT):
                        last = nc.tensor.matmul(ps[:, 4 + i, 0:SEQ], RT[:, k, i * P:(i + 1) * P], keysT[:, k, :],
                                                start=k == 0, stop=k == KT - 1)
                    last.then_inc(s_scores, 1)

            stage(nc.tensor.Fori, step)
            turn_probs(BATCH - 1)
            finish(BATCH - 1, 1)

        @block.scalar
        def _(act):
            def step(b, parity):
                first = isinstance(b, int) and b == 0
                for g in range(TG):
                    dst = (xnT, keysT)[g // (TB * HALVES)]
                    i, h = g // HALVES % TB, g % HALVES
                    act.wait_ge(s_t, TG * b + g + 1)
                    nc.scalar.copy(dst[:, 4 * h:4 * h + 4, i * P:(i + 1) * P],
                                   ps[:, g % 2, :].rearrange("p (k t) -> p k t", k=4)).then_inc(s_tev, 1)
                for o in range(KT):
                    act.wait_ge(s_r, KT * b + o + 1)
                    nc.scalar.activation(RT[:, o, :], ps[:, 2 + o % 2, 0:SEQ], ACT.Identity,
                                         bias=small[:, o:o + 1]).then_inc(s_rev, 1)
                    if o == KT // 2 - 1 and not first:
                        turned_probs(b - 1)
                for i in range(TB):
                    act.wait_ge(s_neg, TB * b + i + 1)
                    nc.scalar.activation(probs[:, i, :], ps[:, 4 + i, 0:SEQ], ACT.Exp, bias=neg[:, i:i + 1],
                                         scale=SCORE_SCALE, accum_out=sums[:, i:i + 1]).then_inc(s_probs, 1)

            def turned_probs(b):
                act.wait_ge(s_pt, b + 1)
                nc.scalar.copy(probsT[:, :, :].rearrange("p k t -> p (k t)"), ps[:, 4, :]).then_inc(s_ptev, 1)

            stage(nc.scalar.Fori, step)
            turned_probs(BATCH - 1)

        @block.vector
        def _(dve):
            seen = [0]

            def link(b, op):
                seen[0] += 1
                op.then_inc(s_self, 1)
                dve.wait_ge(s_self, 5 * TB * b + seen[0])

            def normalise(b):
                for i in range(TB):
                    if not isinstance(b, int) or b >= 1:
                        dve.wait_ge(s_t, TG * (b - 1) + HALVES * (i + 1))
                    nt = TB * b + i
                    nc.vector.tensor_scalar(xn[:, i, :], y[:, bass.ds(nt, 1), :].rearrange("p o d -> p (o d)"),
                                            mv[:, bass.ds(nt, 1), 0], rstd[:, bass.ds(nt, 1)],
                                            ALU.subtract, ALU.mult).then_inc(s_xn, 1)

            def softmax(b, parity):
                seen[0] = 0
                for i in range(TB):
                    dve.wait_ge(s_scores, TB * b + i + 1)
                    link(b, nc.vector.reduce_max(mx[:, i:i + 1], ps[:, 4 + i, 0:SEQ], AX.X))
                    link(b, nc.vector.tensor_tensor(row[:, i:i + 1], ps[:, 4 + i, SEQ:SEQ + 1], small[:, 16:17], ALU.add))
                    link(b, nc.vector.tensor_tensor(top[:, i:i + 1], mx[:, i:i + 1], row[:, i:i + 1], ALU.add))
                    link(b, nc.vector.tensor_tensor(dif[:, i:i + 1], row[:, i:i + 1], top[:, i:i + 1], ALU.subtract))
                    nc.vector.tensor_scalar(neg[:, i:i + 1], dif[:, i:i + 1], SCORE_SCALE, None, ALU.mult).then_inc(s_neg, 1)
                for i in range(TB):
                    dve.wait_ge(s_probs, TB * b + i + 1)
                    link(b, nc.vector.reciprocal(rsum[:, parity, i:i + 1], sums[:, i:i + 1]))

            def residual(b, parity):
                for i in range(TB):
                    tile = y[:, bass.ds(TB * b + i, 1), :].rearrange("p o d -> p (o d)")
                    for h in range(HALVES):
                        n = i * HALVES + h
                        dve.wait_ge(s_att, ATT * b + n + 1)
                        nc.vector.scalar_tensor_tensor(out=tile[:, h * BANK:(h + 1) * BANK], in0=ps[:, 6 + n % 2, :],
                                                       scalar=rsum[:, parity, i:i + 1],
                                                       in1=tile[:, h * BANK:(h + 1) * BANK],
                                                       op0=ALU.mult, op1=ALU.add).then_inc(s_y, 1)

            def step(b, parity):
                first = isinstance(b, int) and b == 0
                if first:
                    normalise(0)
                if not (isinstance(b, int) and b == BATCH - 1):
                    normalise(b + 1)
                if not first:
                    residual(b - 1, 1 - parity)
                softmax(b, parity)

            stage(nc.vector.Fori, step)
            residual(BATCH - 1, 1)


def feed_forward(nc, st, t):
    y, ident, sg, su, sd, ps, mv, rstd = (t[n] for n in ("y", "ident", "sg", "su", "sd", "ps", "mv", "rstd"))
    gate_out, up_out, y_out, out_t = t["gate_out"], t["up_out"], t["y_out"], t["out_t"]

    def sb(name, shape, dt):
        return st.enter_context(nc.sbuf_tensor(name, shape, dt))

    def sem(name):
        return st.enter_context(nc.semaphore(name))

    xT = sb("xT", [P, 2, KT, TOK], F16)
    wgu = sb("wgu", [P, 2, 2, 2, KT, P], F16)
    wd = sb("wd", [P, 3, 2, DIM], F16)
    h = sb("h", [P, 3, 2, TOK], F16)
    act_buf = sb("act_buf", [P, 2, BANK], F32)
    q = sb("q", [P, Q_RING, BANK], I32)
    sq = sb("sq", [P, 2, BANK], F32)
    gate_now = sb("gate_now", [P, 2], F32)
    w = sb("w", [P, P_RING, BANK], F32)
    xn = h[:, 0, :, :].rearrange("p a b -> p (a b)").bitcast(F32).rearrange("p (i d) -> p i d", i=2)
    stats = act_buf[:, 0, 0:NT * 12].rearrange("p (i a b) -> p i a b", i=NT, a=2)
    std = act_buf[:, 1, 0:NT]

    s_q = [sem(f"s_q{i}") for i in range(Q_RING)]
    names = ("s_var", "s_std", "s_rstd", "s_xn", "s_xt", "s_xhi", "s_xlo", "s_act", "s_scaled", "s_fac", "s_turned",
             "s_whi", "s_wlo", "s_g", "s_u", "s_silu", "s_h", "s_hhi", "s_hlo", "s_down", "s_y", "s_out", "s_gate", "s_selfc")
    (s_var, s_std, s_rstd, s_xn, s_xt, s_xhi, s_xlo, s_act, s_scaled, s_fac, s_turned,
     s_whi, s_wlo, s_g, s_u, s_silu, s_h, s_hhi, s_hlo, s_down, s_y, s_out, s_gate, s_self) = (sem(n + "_f") for n in names)
    HALVES = DIM // BANK
    OUT = NT * HALVES
    OPS = NF + 1

    def weights_of(chunk_odd, down_parity, kind):
        mat, half = kind
        if mat < 2:
            return [wgu[:, chunk_odd, mat, part, 4 * half:4 * half + 4, :].rearrange("p k m -> p (k m)") for part in range(2)]
        return [wd[:, slot_of(chunk_odd, down_parity), part, half * BANK:(half + 1) * BANK] for part in range(2)]

    def dest(p_parity, e):
        if e < 4:
            return weights_of(1, 0, (e // 2, e % 2))
        if e < 6:
            return weights_of(0, p_parity, (2, e - 4))
        if e < 10:
            return weights_of(0, 0, ((e - 6) // 2, e % 2))
        return weights_of(1, 0, (2, e - 10))

    def ahead(p, e):
        return (p, e + LEAD) if e + LEAD < EVENTS else (p + 1, e + LEAD - EVENTS)

    def exists(p, e):
        if isinstance(p, int) and p >= PERIODS:
            return False
        return has_unit(p, e)

    def count(p, e):
        u = FIRST_UNITS + EVENTS * p + e
        return u - 4 if isinstance(p, int) and p == PERIODS - 1 and e >= 10 else u

    def periods(eng_loop, period):
        period(0, 0)
        with eng_loop(0, (PERIODS - 2) // 2) as j:
            period(2 * j + 1, 1)
            period(2 * j + 2, 0)
        period(PERIODS - 1, (PERIODS - 1) % 2)

    first_units = [(n, 0, (n // 2, n % 2)) for n in range(FIRST_UNITS)]

    with nc.Block() as block:
        @block.sync
        def _(sp):
            def load(u, ring, pair, chunk, kind):
                mat, half = kind
                if kind != (2, 0):
                    wait(sp, s_act, OPS * (u + pair - Q_RING + 1))
                if mat < 2:
                    src = t[("gate_q", "up_q")[mat]][bass.ds(chunk * P, P), half * BANK:(half + 1) * BANK]
                    sp.dma_start(q[:, ring, :], src).then_inc(s_q[ring], 16)
                else:
                    src = t["down_q"].rearrange("(k p) (c m) -> p k c m", p=P, m=P)[:, 4 * half:4 * half + 4, bass.ds(chunk, 1), :]
                    src = src.rearrange("p k o m -> p k (o m)")
                    sp.dma_start(q[:, ring, :].rearrange("p (k m) -> p k m", k=4), src).then_inc(s_q[ring], 16)

            def period(p, parity):
                for e in range(EVENTS):
                    if exists(p, e):
                        _, chunk, kind = unit_of(p, e)
                        u = count(p, e)
                        if not exists(p, e - 1) and kind == (2, 0):
                            sp.wait_ge(s_act, OPS * (u - Q_RING + 1))
                        load(u, (u if isinstance(u, int) else FIRST_UNITS + e) % Q_RING, e in (3, 9), chunk, kind)

            for n, chunk, kind in first_units:
                load(n, n % Q_RING, 0, chunk, kind)
            periods(nc.sync.Fori, period)
            for n in range(4):
                sp.wait_ge(s_y, OUT * (PERIODS - 1) + (n + 1) * OUT // 4)
                sp.dma_start(out_t[:, 4 * n:4 * n + 4, :], y[:, 4 * n:4 * n + 4, :]).then_inc(s_out, 16)
            sp.wait_ge(s_out, 64)

        @block.gpsimd
        def _(pool):
            def scale_unit(u, slot, chunk, kind):
                mat, half = kind
                pool.wait_ge(s_act, OPS * u + 1)
                if mat < 2:
                    tile = w[:, slot, :].rearrange("p (b j) -> p b j", j=QBLOCK)
                    s = (sg, su)[mat][:, bass.ds(chunk, 1), half * KB // 2:(half + 1) * KB // 2]
                    s = s.rearrange("p o b -> p (o b)").rearrange("p (b j) -> p b j", j=1).broadcast_to([P, KB // 2, QBLOCK])
                else:
                    tile = w[:, slot, :].rearrange("p (k b j) -> p k b j", k=4, j=QBLOCK)
                    s = sd[:, 4 * half:4 * half + 4, bass.ds(chunk * 2, 2)]
                    s = s.rearrange("p k (b j) -> p k b j", j=1).broadcast_to([P, 4, 2, QBLOCK])
                nc.gpsimd.tensor_tensor(tile, tile, s, ALU.mult).then_inc(s_scaled, 1)

            def hidden_lo(p, parity, e):
                odd, n = GU_EVENT[e]
                b = NBLK * (2 * p + odd) + n
                pool.wait_ge(s_hhi, b + 1)
                cols = slice(n * BANK, (n + 1) * BANK)
                s = slot_of(odd, parity)
                nc.gpsimd.tensor_tensor(h[:, s, 1, cols], act_buf[:, n % 2, :], h[:, s, 0, cols], ALU.subtract).then_inc(s_hlo, 1)

            def period(p, parity):
                for e in range(EVENTS):
                    p2, e2 = ahead(p, e)
                    if exists(p2, e2):
                        _, chunk, kind = unit_of(p2, e2)
                        u = count(p2, e2)
                        scale_unit(u, (u if isinstance(u, int) else FIRST_UNITS + e2) % P_RING, chunk, kind)
                    if e in GU_EVENT:
                        hidden_lo(p, parity, e)

            for n, chunk, kind in first_units:
                scale_unit(n, n % P_RING, chunk, kind)
            for e in range(LEAD):
                u, chunk, kind = unit_of(0, e)
                scale_unit(u, u % P_RING, chunk, kind)
            periods(nc.gpsimd.Fori, period)

        @block.scalar
        def _(act):
            def look_up(u, slot, ring, q_count, ops):
                for i in ops:
                    if i == 0:
                        act.wait_ge(s_q[ring], q_count)
                        wait(act, s_turned, u - P_RING + 1)
                        nc.scalar.activation(w[:, slot, :], q[:, ring, :], ACT.Copy, bias=-ZERO_CODE).then_inc(s_act, 1)
                        continue
                    n = NF * u + i - 1
                    wait(act, s_fac, n - 1)
                    a, b, _ = FACTORS[i - 1]
                    nc.scalar.activation(sq[:, sq_slot[0], :], q[:, ring, :], ACT.Square, bias=b,
                                         scale=a).then_inc(s_act, 1)
                    sq_slot[0] ^= 1

            sq_slot = [0]

            def unit_args(p, e):
                u = count(p, e)
                k = u if isinstance(u, int) else FIRST_UNITS + e
                if isinstance(u, int):
                    return u, u % P_RING, u % Q_RING, 16 * (u // Q_RING + 1)
                return u, k % P_RING, k % Q_RING, 16 * (k // Q_RING + 1) + 16 * (EVENTS // Q_RING) * p

            def weights_hi(p, parity, e):
                u = count(p, e)
                act.wait_ge(s_turned, u + 1)
                nc.scalar.copy(dest(parity, e)[0], ps[:, e % 2, :]).then_inc(s_whi, 1)

            def silu(p, e):
                odd, n = GU_EVENT[e]
                b = NBLK * (2 * p + odd) + n
                act.wait_ge(s_g, b + 1)
                wait(act, s_hlo, b - 1)
                if e == 0:
                    act.wait_ge(s_gate, p + 1)
                nc.scalar.activation(act_buf[:, n % 2, :], ps[:, 2 + n % 2, :], ACT.Silu,
                                     scale=gate_now[:, odd:odd + 1]).then_inc(s_silu, 1)

            def hidden_hi(p, parity, e):
                odd, n = GU_EVENT[e]
                act.wait_ge(s_h, NBLK * (2 * p + odd) + n + 1)
                nc.scalar.copy(h[:, slot_of(odd, parity), 0, n * BANK:(n + 1) * BANK], act_buf[:, n % 2, :]).then_inc(s_hhi, 1)

            def period(p, parity):
                for e in range(EVENTS):
                    p2, e2 = ahead(p, e)
                    args = unit_args(p2, e2) if exists(p2, e2) else None
                    if args:
                        look_up(*args, range(0, OPS // 2))
                    if e in GU_EVENT:
                        silu(p, e)
                    if args:
                        look_up(*args, range(OPS // 2, OPS))
                    if e in GU_EVENT:
                        hidden_hi(p, parity, e)
                    if exists(p, e):
                        weights_hi(p, parity, e)

            act.wait_ge(s_var, 1)
            nc.scalar.activation(std, rstd[:, :], ACT.Sqrt).then_inc(s_std, 1)
            for n in range(2 * NT):
                act.wait_ge(s_xt, n + 1)
                nc.scalar.copy(x_part(xT, n, 0), ps[:, n % 2, :].rearrange("p (k t) -> p k t", k=4)).then_inc(s_xhi, 1)
            for n in range(FIRST_UNITS):
                look_up(n, n % P_RING, n % Q_RING, 16 * (n // Q_RING + 1), range(OPS))
                act.wait_ge(s_turned, n + 1)
                nc.scalar.copy(weights_of(0, 0, (n // 2, n % 2))[0], ps[:, n % 2, :]).then_inc(s_whi, 1)
            for e in range(LEAD):
                look_up(*unit_args(0, e), range(OPS))
            periods(nc.scalar.Fori, period)

        @block.vector
        def _(dve):
            def factors(u, slot, ops):
                for i in ops:
                    if i == 0:
                        dve.wait_ge(s_scaled, u + 1)
                    else:
                        dve.wait_ge(s_fac, NF * u + i)
                    dve.wait_ge(s_act, OPS * u + i + 2)
                    nc.vector.scalar_tensor_tensor(out=w[:, slot, :], in0=sq[:, sq_slot[0], :], scalar=FACTORS[i][2],
                                                   in1=w[:, slot, :], op0=ALU.add, op1=ALU.mult).then_inc(s_fac, 1)
                    sq_slot[0] ^= 1
                    yield

            sq_slot = [0]

            def weights_lo(p, parity, e):
                hi, lo = dest(parity, e)
                dve.wait_ge(s_whi, count(p, e) + 1)
                nc.vector.tensor_tensor(lo, ps[:, e % 2, :], hi, ALU.subtract).then_inc(s_wlo, 1)

            def hidden(p, e):
                odd, n = GU_EVENT[e]
                b = NBLK * (2 * p + odd) + n
                dve.wait_ge(s_u, b + 1)
                dve.wait_ge(s_silu, b + 1)
                nc.vector.scalar_tensor_tensor(out=act_buf[:, n % 2, :], in0=ps[:, 4 + n % 2, :],
                                               scalar=up_out[:, bass.ds(2 * p + odd, 1)], in1=act_buf[:, n % 2, :],
                                               op0=ALU.mult, op1=ALU.mult).then_inc(s_h, 1)

            def add_down(p, n):
                i, hh = n // HALVES, n % HALVES
                cols = slice(hh * BANK, (hh + 1) * BANK)
                dve.wait_ge(s_down, OUT * p + n + 1)
                nc.vector.scalar_tensor_tensor(out=y[:, i, cols], in0=ps[:, 6 + n % 2, :], scalar=y_out[:, 0:1],
                                               in1=y[:, i, cols], op0=ALU.mult, op1=ALU.add).then_inc(s_y, 1)

            def period(p, parity):
                wait(dve, s_silu, 2 * NBLK * p)
                nc.vector.tensor_copy(gate_now[:, :], gate_out[:, bass.ds(2 * p, 2)]).then_inc(s_gate, 1)
                for e in range(EVENTS):
                    p2, e2 = ahead(p, e)
                    todo = iter(())
                    if exists(p2, e2):
                        u = count(p2, e2)
                        todo = factors(u, (u if isinstance(u, int) else FIRST_UNITS + e2) % P_RING, range(NF))
                    if e in DOWN_EVENT and not (isinstance(p, int) and p == 0):
                        for n in range(OUT // 4):
                            add_down(p - 1, DOWN_EVENT[e] * OUT // 4 + n)
                            next(todo, None)
                    for _ in todo:
                        pass
                    if e in GU_EVENT:
                        hidden(p, e)
                    if exists(p, e):
                        weights_lo(p, parity, e)

            seen = [0]

            def link(op):
                seen[0] += 1
                op.then_inc(s_self, 1)
                dve.wait_ge(s_self, seen[0])

            for i in range(NT):
                nc.vector.bn_stats(stats[:, i, 0, :], y[:, i, 0:BANK])
                link(nc.vector.bn_stats(stats[:, i, 1, :], y[:, i, BANK:DIM]))
            for i in range(NT):
                last = nc.vector.bn_aggr(mv[:, i, :], stats[:, i, :, :].rearrange("p a b -> p (a b)"))
            link(last)
            nc.vector.tensor_scalar(rstd[:, :], mv[:, :, 1], EPS, None, ALU.add).then_inc(s_var, 1)
            dve.wait_ge(s_std, 1)
            link(nc.vector.reciprocal(rstd[:, :], std))
            link(nc.vector.tensor_scalar(rstd[:, :], rstd[:, :], X_SCALE, None, ALU.mult))

            def norm(i):
                wait(dve, s_xt, 2 * (i - 1))
                nc.vector.tensor_scalar(xn[:, i % 2, :], y[:, i, :], mv[:, i, 0:1], rstd[:, i:i + 1],
                                        ALU.subtract, ALU.mult).then_inc(s_xn, 1)

            norm(0)
            for n in range(2 * NT):
                if n % 2 == 0 and n // 2 + 1 < NT:
                    norm(n // 2 + 1)
                dve.wait_ge(s_xhi, n + 1)
                nc.vector.tensor_tensor(x_part(xT, n, 1), ps[:, n % 2, :].rearrange("p (k t) -> p k t", k=4),
                                        x_part(xT, n, 0), ALU.subtract).then_inc(s_xlo, 1)
            for n in range(FIRST_UNITS):
                for _ in factors(n, n % P_RING, range(NF)):
                    pass
                hi, lo = weights_of(0, 0, (n // 2, n % 2))
                dve.wait_ge(s_whi, n + 1)
                nc.vector.tensor_tensor(lo, ps[:, n % 2, :], hi, ALU.subtract).then_inc(s_wlo, 1)
            for e in range(LEAD):
                u = count(0, e)
                for _ in factors(u, u % P_RING, range(NF)):
                    pass
            periods(nc.vector.Fori, period)
            for n in range(OUT):
                add_down(PERIODS - 1, n)

        @block.tensor
        def _(pe):
            def turn(u, slot, bank):
                pe.wait_ge(s_fac, NF * (u + 1))
                wait(pe, s_wlo, u - 1)
                for k in range(4):
                    last = nc.tensor.transpose(ps[:, bank, k * P:(k + 1) * P], w[:, slot, k * P:(k + 1) * P], ident[:, :])
                last.then_inc(s_turned, 1)

            PARTS = ((0, 0), (0, 1), (1, 0))

            def gate_up(p, e):
                odd, n = GU_EVENT[e]
                b = NBLK * (2 * p + odd) + n
                wait(pe, s_h, b - 1)
                for mat, done in ((0, s_g), (1, s_u)):
                    for k in range(KT):
                        for j, (a, c) in enumerate(PARTS):
                            last = nc.tensor.matmul(ps[:, 2 + 2 * mat + n % 2, :], wgu[:, odd, mat, a, k, :],
                                                    xT[:, c, k, n * BANK:(n + 1) * BANK],
                                                    start=k == 0 and j == 0, stop=k == KT - 1 and j == 2)
                    last.then_inc(done, 1)

            def down(p, parity, n):
                i, hh = n // HALVES, n % HALVES
                if n >= 2:
                    pe.wait_ge(s_y, OUT * p + n - 1)
                todo = [(s, a, c) for s in (slot_of(0, parity), slot_of(1, parity)) for a, c in PARTS]
                for m, (s, a, c) in enumerate(todo):
                    last = nc.tensor.matmul(ps[:, 6 + n % 2, :], h[:, s, a, i * P:(i + 1) * P],
                                            wd[:, s, c, hh * BANK:(hh + 1) * BANK], start=m == 0, stop=m == len(todo) - 1)
                last.then_inc(s_down, 1)

            def down_ready(p):
                pe.wait_ge(s_hlo, NBLK * (2 * p + 2))
                pe.wait_ge(s_wlo, count(p, EVENTS - 1) + 1)

            def period(p, parity):
                for e in range(EVENTS):
                    if e == 0:
                        pe.wait_ge(s_wlo, FIRST_UNITS + EVENTS * (p - 1) + 10 if not isinstance(p, int) or p else FIRST_UNITS)
                    if e == 8:
                        pe.wait_ge(s_wlo, FIRST_UNITS + EVENTS * p + 4)
                    if e in GU_EVENT:
                        gate_up(p, e)
                    elif not (isinstance(p, int) and p == 0):
                        if e == 4:
                            down_ready(p - 1)
                        for n in range(OUT // 4):
                            down(p - 1, 1 - parity, DOWN_EVENT[e] * OUT // 4 + n)
                    if exists(p, e):
                        u = count(p, e)
                        turn(u, (u if isinstance(u, int) else FIRST_UNITS + e) % P_RING, e % 2)

            for n in range(2 * NT):
                pe.wait_ge(s_xn, n // 2 + 1)
                wait(pe, s_xlo, n - 1)
                for k in range(4):
                    src = xn[:, n // 2 % 2, (n % 2 * 4 + k) * P:(n % 2 * 4 + k + 1) * P]
                    last = nc.tensor.transpose(ps[:, n % 2, k * P:(k + 1) * P], src, ident[:, :])
                last.then_inc(s_xt, 1)
            pe.wait_ge(s_xlo, 2 * NT)
            for n in range(FIRST_UNITS):
                turn(n, n % P_RING, n % 2)
            periods(nc.tensor.Fori, period)
            last_pair = PERIODS - 1
            down_ready(last_pair)
            for n in range(OUT):
                down(last_pair, last_pair % 2, n)


def x_part(xT, n, part):
    i, half = n // 2, n % 2
    return xT[:, part, 4 * half:4 * half + 4, i * P:(i + 1) * P]


_INS = ["x", "ctx_4096", "L0_xattn_Wq", "L0_xattn_bq", "L0_xattn_Wk", "L0_xattn_bk", "L0_ffn_gate_q",
        "L0_ffn_gate_absmax", "L0_ffn_up_q", "L0_ffn_up_absmax", "L0_ffn_down_q", "L0_ffn_down_absmax"]


def kernel(**inputs):
    import concourse.bacc as bacc
    from concourse.bass_utils import run_bass_kernel_spmd

    nc = bacc.Bacc("TRN2", target_bir_lowering=False, num_devices=1)
    arrays, args = {}, []
    for name in _INS:
        a = np.ascontiguousarray(inputs[name])
        arrays[f"in_{name}"] = a
        args.append(nc.dram_tensor(f"in_{name}", a.shape, mybir.dt.from_np(a.dtype), kind="ExternalInput").ap())
    args.append(nc.dram_tensor("out_0", (BATCH, SEQ, DIM), F32, kind="ExternalOutput").ap())
    xattn_ffn_kernel(nc, *args)
    r = run_bass_kernel_spmd(nc, [arrays], core_ids=[0])
    return r.results[0]["out_0"]
```

```python
from contextlib import ExitStack

import numpy as np

import concourse.bass as bass
from concourse import mybir

ALU = mybir.AluOpType
ACT = mybir.ActivationFunctionType
AX = mybir.AxisListType
F32 = mybir.dt.float32
F16 = mybir.dt.float16
I32 = mybir.dt.int32

P = 128
BANK = 512
BATCH, SEQ, DIM = 8, 256, 1024
HID = 3584
QBLOCK = 64
TOK = BATCH * SEQ
KT = DIM // P
NT = TOK // P
TB = SEQ // P
CH = HID // P
KB = DIM // QBLOCK
MB = HID // QBLOCK
EPS = 1e-5
SCORE_SCALE = float(DIM) ** -0.5

X_SCALE = 1024.0
W_SCALE = 1024.0
H_BOUND_SCALE = 2.0 ** -5
A_BOUND = 2.0 ** 15
TINY = 1e-15
RSQRT_SEED = 0x5F3759DF
NEWTON_STEPS = 3

ZERO_CODE = 7.0
FACTORS = [
    (0.16843146085739136, -2.5078866481781006, 0.005980083718895912),
    (0.16843146085739136, -1.8140839338302612, 0.1702844202518463),
    (0.16843146085739136, -2.2222657203674316, 0.07722912728786469),
    (0.16843144595623016, -0.31645941734313965, 0.07142763584852219),
    (0.16843146085739136, -0.7382349967956543, 0.15366360545158386),
    (0.16843147575855255, -1.310221791267395, 0.17072737216949463),
    (0.16843146085739136, -0.024128910154104233, 0.005195258650928736),
]
NF = len(FACTORS)
OPS = NF + 1

GU_EVENT = {0: (0, 0), 1: (0, 1), 2: (0, 2), 3: (0, 3), 8: (1, 0), 9: (1, 1), 10: (1, 2), 11: (1, 3)}
DOWN_EVENT = {4: 0, 5: 1, 6: 2, 7: 3}
EVENTS = 12
PERIODS = CH // 2
FIRST_UNITS = 4
UNITS = 6 * CH
LEAD = 2
NBLK = TOK // BANK
Q_RING, P_RING = 3, 3
EARLY_UNITS = 3


def unit_of(p, e):
    u = FIRST_UNITS + EVENTS * p + e
    if e < 4:
        return u, 2 * p + 1, (e // 2, e % 2)
    if e < 6:
        return u, 2 * p, (2, e - 4)
    if e < 10:
        return u, 2 * p + 2, ((e - 6) // 2, e % 2)
    return u, 2 * p + 1, (2, e - 10)


def has_unit(p, e):
    return not (isinstance(p, int) and p == PERIODS - 1 and 6 <= e < 10)


def slot_of(odd, parity):
    return 1 if odd else 2 * parity


def wait(eng, sem, count):
    if not isinstance(count, int) or count > 0:
        eng.wait_ge(sem, count)


PARTS = ((0, 0), (0, 1), (1, 0))


def rsqrt(nc, out, var, guess, tmp, link):
    link(nc.vector.tensor_scalar(tmp, var, EPS, None, ALU.add))
    link(nc.vector.tensor_single_scalar(guess.bitcast(I32), tmp.bitcast(I32), 1, ALU.logical_shift_right))
    link(nc.vector.tensor_scalar(out.bitcast(I32), guess.bitcast(I32), -1.0, float(RSQRT_SEED), ALU.mult, ALU.add))
    for _ in range(NEWTON_STEPS):
        link(nc.vector.tensor_tensor(guess, out, out, ALU.mult))
        link(nc.vector.tensor_tensor(guess, guess, tmp, ALU.mult))
        link(nc.vector.tensor_scalar(guess, guess, -0.5, 1.5, ALU.mult, ALU.add))
        link(nc.vector.tensor_tensor(out, out, guess, ALU.mult))


class Shared:
    pass


class Units:

    def __init__(self, nc, stack):
        def sb(name, shape, dt):
            return stack.enter_context(nc.sbuf_tensor(name, shape, dt))

        def sem(name):
            return stack.enter_context(nc.semaphore(name))

        self.q = sb("q", [P, Q_RING, BANK], I32)
        self.sq = sb("sq", [P, 2, BANK], F32)
        self.w = sb("w", [P, P_RING, BANK], F32)
        self.wgu = sb("wgu", [P, 2, 2, 2, KT, P], F16)
        self.s_q = [sem(f"s_q{i}") for i in range(Q_RING)]
        self.s_act = sem("s_act")
        self.s_scaled = sem("s_scaled")
        self.s_fac = sem("s_fac")
        self.s_turned = sem("s_turned")
        self.s_whi = sem("s_whi")
        self.s_wlo = sem("s_wlo")


def load_unit(nc, eng, un, t, u, ring, chunk, kind):
    mat, half = kind
    if mat < 2:
        src = (t.gate_q, t.up_q)[mat][bass.ds(chunk * P, P), half * BANK:(half + 1) * BANK]
        eng.dma_start(un.q[:, ring, :], src).then_inc(un.s_q[ring], 16)
    else:
        src = t.down_q.rearrange("(k p) (c m) -> p k c m", p=P, m=P)[:, 4 * half:4 * half + 4, bass.ds(chunk, 1), :]
        src = src.rearrange("p k o m -> p k (o m)")
        eng.dma_start(un.q[:, ring, :].rearrange("p (k m) -> p k m", k=4), src).then_inc(un.s_q[ring], 16)


def scale_unit(nc, pool, un, t, u, slot, chunk, kind):
    mat, half = kind
    pool.wait_ge(un.s_act, OPS * u + 1)
    if mat < 2:
        tile = un.w[:, slot, :].rearrange("p (b j) -> p b j", j=QBLOCK)
        s = (t.sg, t.su)[mat][:, bass.ds(chunk, 1), half * KB // 2:(half + 1) * KB // 2]
        s = s.rearrange("p o b -> p (o b)").rearrange("p (b j) -> p b j", j=1).broadcast_to([P, KB // 2, QBLOCK])
    else:
        tile = un.w[:, slot, :].rearrange("p (k b j) -> p k b j", k=4, j=QBLOCK)
        s = t.sd[:, 4 * half:4 * half + 4, bass.ds(chunk * 2, 2)]
        s = s.rearrange("p k (b j) -> p k b j", j=1).broadcast_to([P, 4, 2, QBLOCK])
    nc.gpsimd.tensor_tensor(tile, tile, s, ALU.mult).then_inc(un.s_scaled, 1)


def look_up(nc, act, un, u, slot, ring, q_count, even, ops):
    for i in ops:
        if i == 0:
            act.wait_ge(un.s_q[ring], q_count)
            wait(act, un.s_turned, u - P_RING + 1)
            nc.scalar.activation(un.w[:, slot, :], un.q[:, ring, :], ACT.Copy, bias=-ZERO_CODE).then_inc(un.s_act, 1)
        else:
            wait(act, un.s_fac, NF * u + i - 2)
            a, b, _ = FACTORS[i - 1]
            nc.scalar.activation(un.sq[:, (i - even) % 2, :], un.q[:, ring, :], ACT.Square, bias=b,
                                 scale=a).then_inc(un.s_act, 1)


def factors(nc, dve, un, u, slot, even):
    for i in range(NF):
        if i == 0:
            dve.wait_ge(un.s_scaled, u + 1)
        else:
            dve.wait_ge(un.s_fac, NF * u + i)
        dve.wait_ge(un.s_act, OPS * u + i + 2)
        nc.vector.scalar_tensor_tensor(out=un.w[:, slot, :], in0=un.sq[:, (i + 1 - even) % 2, :], scalar=FACTORS[i][2],
                                       in1=un.w[:, slot, :], op0=ALU.add, op1=ALU.mult).then_inc(un.s_fac, 1)
        yield


def turn_unit(nc, pe, un, t, u, slot, bank):
    pe.wait_ge(un.s_fac, NF * (u + 1))
    for k in range(4):
        last = nc.tensor.transpose(t.ps[:, bank, k * P:(k + 1) * P], un.w[:, slot, k * P:(k + 1) * P], t.ident[:, :])
    last.then_inc(un.s_turned, 1)


def keep_hi(nc, act, un, t, u, dst, bank):
    act.wait_ge(un.s_turned, u + 1)
    nc.scalar.copy(dst, t.ps[:, bank, :]).then_inc(un.s_whi, 1)


def keep_lo(nc, dve, un, t, u, hi, lo, bank):
    dve.wait_ge(un.s_whi, u + 1)
    nc.vector.tensor_tensor(lo, t.ps[:, bank, :], hi, ALU.subtract).then_inc(un.s_wlo, 1)


def gate_up_dest(un, odd, mat, half):
    return [un.wgu[:, odd, mat, part, 4 * half:4 * half + 4, :].rearrange("p k m -> p (k m)") for part in range(2)]


def xattn_ffn_kernel(nc, x, ctx, Wq, bq, Wk, bk, gate_q, gate_absmax, up_q, up_absmax, down_q, down_absmax, out):
    with ExitStack() as whole:
        def sb(name, shape, dt):
            return whole.enter_context(nc.sbuf_tensor(name, shape, dt))

        t = Shared()
        t.ctx, t.Wq, t.bq, t.Wk, t.bk = ctx, Wq, bq, Wk, bk
        t.gate_q, t.up_q, t.down_q = gate_q, up_q, down_q
        t.gate_absmax, t.up_absmax, t.down_absmax = gate_absmax, up_absmax, down_absmax
        t.x_t = x.rearrange("b (t p) d -> p (b t) d", p=P)
        t.out_t = out.rearrange("b (t p) d -> p (b t) d", p=P)
        t.y = sb("y", [P, NT, DIM], F32)
        t.ident = sb("ident", [P, P], F32)
        t.sg = sb("sg", [P, CH, KB], F32)
        t.su = sb("su", [P, CH, KB], F32)
        t.sd = sb("sd", [P, KT, MB], F32)
        t.gate_out = sb("gate_out", [P, CH], F32)
        t.up_out = sb("up_out", [P, CH], F32)
        t.y_out = sb("y_out", [P, 1], F32)
        t.mv = sb("mv", [P, NT, 2], F32)
        t.rstd = sb("rstd", [P, NT], F32)
        t.guess = sb("guess", [P, NT], F32)
        t.var = sb("var", [P, NT], F32)
        t.ps = whole.enter_context(nc.psum_tensor("ps", [P, 8, BANK], F32))
        un = Units(nc, whole)
        with ExitStack() as attn:
            def sba(name, shape, dt):
                return attn.enter_context(nc.sbuf_tensor(name, shape, dt))

            t.A = sba("A", [P, 2, KT, DIM], F16)
            t.a_in = sba("a_in", [P, 1], F32)
            t.a_out = sba("a_out", [P, 1], F32)
            t.key_row = sba("key_row", [P, DIM], F32)
            t.query_col = sba("query_col", [P, KT], F32)
            t.bias_dot = sba("bias_dot", [P, 1], F32)
            prepare(nc, t, un)
            attend(nc, t, un)
        feed_forward(nc, t, un)


def prepare(nc, t, un):
    with ExitStack() as st:
        def sb(name, shape, dt):
            return st.enter_context(nc.sbuf_tensor(name, shape, dt))

        def sem(name):
            return st.enter_context(nc.semaphore(name))

        ps, y = t.ps, t.y
        HALVES = DIM // BANK
        XQ = 4
        wq = sb("wq", [P, KT, DIM], F32)
        wk = sb("wk", [P, KT, DIM], F32)
        bqk = sb("bqk", [P, 2, KT], F32)
        prod = sb("prod", [P, KT], F32)
        bsum = sb("bsum", [P, 1], F32)
        ones = sb("ones", [P, P], F32)
        stats = sb("stats", [P, 2, 2, 6], F32)
        Sg = sb("Sg", [P, CH], F32)
        Su = sb("Su", [P, CH], F32)
        Rs = sb("Rs", [P, CH], F32)
        wmax = sb("wmax", [P, 2, KT], F32)
        top = sb("top", [P, 4], F32)
        topall = sb("topall", [P, 4], F32)
        rtop = sb("rtop", [P, 4], F32)
        sums = un.wgu[:, 1, :, :, :, :].rearrange("p m a k c -> p (m a k c)").bitcast(F32).rearrange("p (m d) -> p m d", m=2)
        s_w = [sem(f"s_w{k}") for k in range(KT)]
        s_wk2 = [sem(f"s_wk2{k}") for k in range(KT)]
        s_x = [sem(f"s_x{k}") for k in range(XQ)]
        s_b, s_abs, s_id, s_scales, s_sums, s_rows = (sem(n) for n in ("s_b", "s_abs", "s_id", "s_scales", "s_sums", "s_rows"))
        s_acc, s_ahi, s_alo, s_top, s_topall, s_ain, s_self = (
            sem(n) for n in ("s_acc", "s_ahi", "s_alo", "s_top", "s_topall", "s_ain", "s_self"))
        first = [(n, 0, (n // 2, n % 2)) for n in range(EARLY_UNITS)]
        UNIT_BANK = 5

        with nc.Block() as block:
            @block.sync
            def _(sp):
                for k in range(KT):
                    rows = slice(k * P, (k + 1) * P)
                    sp.dma_start(wq[:, k, :], t.Wq[rows, :]).then_inc(s_w[k], 16)
                    sp.dma_start(wk[:, k, 0:BANK], t.Wk[rows, 0:BANK]).then_inc(s_w[k], 16)
                for k in range(KT):
                    sp.dma_start(wk[:, k, BANK:DIM], t.Wk[k * P:(k + 1) * P, BANK:DIM]).then_inc(s_wk2[k], 16)
                for n in range(XQ):
                    tiles = slice(n * NT // XQ, (n + 1) * NT // XQ)
                    sp.dma_start(y[:, tiles, :], t.x_t[:, tiles, :]).then_inc(s_x[n], 16)

            @block.scalar
            def _(act):
                act.dma_start(t.sg[:, :, :], t.gate_absmax.rearrange("(c p b) -> p c b", p=P, b=KB)).then_inc(s_abs, 16)
                act.dma_start(t.su[:, :, :], t.up_absmax.rearrange("(c p b) -> p c b", p=P, b=KB)).then_inc(s_abs, 16)
                act.dma_start(t.sd[:, :, :], t.down_absmax.rearrange("(k p b) -> p k b", p=P, b=MB)).then_inc(s_abs, 16)
                act.dma_start(bqk[:, 0, :], t.bq.rearrange("(k p) -> p k", p=P),
                              allow_slow_non_contiguous=True).then_inc(s_b, 16)
                act.dma_start(bqk[:, 1, :], t.bk.rearrange("(k p) -> p k", p=P),
                              allow_slow_non_contiguous=True).then_inc(s_b, 16)
                for n, chunk, kind in first:
                    load_unit(nc, act, un, t, n, n % Q_RING, chunk, kind)
                for n, chunk, kind in first:
                    look_up(nc, act, un, n, n % P_RING, n % Q_RING, 16 * (n // Q_RING + 1), n % 2 == 0, range(OPS))
                act.wait_ge(s_ain, 1)
                for h in range(HALVES):
                    for i in range(KT):
                        act.wait_ge(s_acc, h * KT + i + 1)
                        nc.scalar.activation(t.A[:, 0, i, h * BANK:(h + 1) * BANK], ps[:, i, :], ACT.Copy,
                                             scale=t.a_in[:, 0:1]).then_inc(s_ahi, 1)
                for n, chunk, kind in first:
                    keep_hi(nc, act, un, t, n, gate_up_dest(un, 0, *kind)[0], UNIT_BANK + n % 2)

            @block.gpsimd
            def _(pool):
                nc.gpsimd.memset(t.ident[:, :], 0.0).then_inc(s_id, 1)
                nc.gpsimd.memset(ones[:, :], 1.0).then_inc(s_id, 1)
                pool.wait_ge(s_id, 2)
                nc.gpsimd.affine_select(out=t.ident[:, :], in_=t.ident[:, :], compare_op=ALU.not_equal, fill=1.0, base=0,
                                        pattern=[[-1, P]], channel_multiplier=1).then_inc(s_id, 1)
                pool.wait_ge(s_top, 1)
                nc.gpsimd.partition_all_reduce(topall[:, 0:2], top[:, 0:2], P, bass.bass_isa.ReduceOp.max).then_inc(s_topall, 1)
                pool.wait_ge(s_scales, 1)
                for n, chunk, kind in first:
                    scale_unit(nc, pool, un, t, n, n % P_RING, chunk, kind)
                pool.wait_ge(s_top, 2)
                nc.gpsimd.partition_all_reduce(topall[:, 2:4], top[:, 2:4], P, bass.bass_isa.ReduceOp.max).then_inc(s_topall, 1)

            @block.tensor
            def _(pe):
                for h in range(HALVES):
                    for k in range(KT):
                        pe.wait_ge((s_w, s_wk2)[h][k], (32, 16)[h])
                        for i in range(KT):
                            if h and k == 0:
                                pe.wait_ge(s_alo, i + 1)
                            last = nc.tensor.matmul(ps[:, i, :], wq[:, k, i * P:(i + 1) * P],
                                                    wk[:, k, h * BANK:(h + 1) * BANK], start=k == 0, stop=k == KT - 1)
                            if k == KT - 1:
                                last.then_inc(s_acc, 1)
                pe.wait_ge(s_alo, KT + 3)
                pe.wait_ge(s_sums, 1)
                for h in range(HALVES):
                    nc.tensor.matmul(ps[:, h, :], ones[:, :], sums[:, 0, h * BANK:(h + 1) * BANK], start=True, stop=True)
                for i in range(KT):
                    nc.tensor.matmul(ps[:, 2, i:i + 1], sums[:, 1, i * P:(i + 1) * P], ones[:, 0:1], start=True, stop=True)
                nc.tensor.matmul(ps[:, 2, KT:KT + 1], ones[:, :], bsum[:, :], start=True, stop=True).then_inc(s_rows, 1)
                pe.wait_ge(s_alo, KT + UNIT_BANK + 2)
                pe.wait_ge(s_id, 3)
                for n, _, _ in first:
                    wait(pe, un.s_wlo, n - 1)
                    turn_unit(nc, pe, un, t, n, n % P_RING, UNIT_BANK + n % 2)

            @block.vector
            def _(dve):
                done = [0]

                def link(op):
                    done[0] += 1
                    op.then_inc(s_self, 1)
                    dve.wait_ge(s_self, done[0])

                def lo_parts(h):
                    for i in range(KT):
                        dve.wait_ge(s_ahi, h * KT + i + 1)
                        cols = slice(h * BANK, (h + 1) * BANK)
                        nc.vector.scalar_tensor_tensor(out=t.A[:, 1, i, cols], in0=ps[:, i, :], scalar=t.a_in[:, 0:1],
                                                       in1=t.A[:, 0, i, cols], op0=ALU.mult, op1=ALU.subtract).then_inc(s_alo, 1)

                dve.wait_ge(s_abs, 48)
                for n, (S, s) in enumerate(((Sg, t.sg), (Su, t.su))):
                    link(nc.vector.tensor_reduce(S[:, :], s[:, :, :], axis=AX.X, op=ALU.max, apply_absolute_value=True))
                    link(nc.vector.tensor_scalar(S[:, :], S[:, :], TINY, None, ALU.max))
                    link(nc.vector.reciprocal(Rs[:, :], S[:, :]))
                    link(nc.vector.tensor_scalar(Rs[:, :], Rs[:, :], W_SCALE, None, ALU.mult))
                    link(nc.vector.tensor_tensor(s[:, :, :], s[:, :, :],
                                                 Rs[:, :].rearrange("p (c o) -> p c o", o=1).broadcast_to([P, CH, KB]), ALU.mult))
                nc.vector.tensor_scalar(t.gate_out[:, :], Sg[:, :], 1.0 / (X_SCALE * W_SCALE), None,
                                        ALU.mult).then_inc(s_scales, 1)
                link(nc.vector.tensor_tensor(Rs[:, :], Sg[:, :], Su[:, :], ALU.mult))
                link(nc.vector.tensor_reduce(top[:, 0:1], Rs[:, :], axis=AX.X, op=ALU.max))
                link(nc.vector.tensor_reduce(top[:, 1:2], t.sd[:, :, :], axis=AX.XY, op=ALU.max, apply_absolute_value=True))
                nc.vector.tensor_scalar(top[:, 1:2], top[:, 1:2], TINY, None, ALU.max).then_inc(s_top, 1)
                for n, _, _ in first:
                    for _ in factors(nc, dve, un, n, n % P_RING, n % 2 == 0):
                        pass
                for k in range(KT):
                    dve.wait_ge(s_w[k], 32)
                    nc.vector.tensor_reduce(wmax[:, 0, k:k + 1], wq[:, k, :], axis=AX.X, op=ALU.max, apply_absolute_value=True)
                for k in range(KT):
                    dve.wait_ge(s_wk2[k], 16)
                    last = nc.vector.tensor_reduce(wmax[:, 1, k:k + 1], wk[:, k, :], axis=AX.X, op=ALU.max,
                                                   apply_absolute_value=True)
                link(last)
                link(nc.vector.tensor_reduce(top[:, 2:4], wmax[:, :, :], axis=AX.X, op=ALU.max))
                nc.vector.tensor_scalar(top[:, 2:4], top[:, 2:4], TINY, None, ALU.max).then_inc(s_top, 1)
                dve.wait_ge(s_topall, 2)
                link(nc.vector.reciprocal(rtop[:, :], topall[:, :]))
                link(nc.vector.tensor_scalar(t.a_in[:, :], rtop[:, 2:3], rtop[:, 3:4], None, ALU.mult))
                nc.vector.tensor_scalar(t.a_in[:, :], t.a_in[:, :], A_BOUND / DIM, None, ALU.mult).then_inc(s_ain, 1)
                link(nc.vector.tensor_scalar(t.a_out[:, :], topall[:, 2:3], topall[:, 3:4], None, ALU.mult))
                nc.vector.tensor_scalar(t.a_out[:, :], t.a_out[:, :], DIM / (A_BOUND * X_SCALE), None, ALU.mult)
                nc.vector.tensor_scalar(t.up_out[:, :], Su[:, :], rtop[:, 0:1], H_BOUND_SCALE / (X_SCALE * W_SCALE),
                                        ALU.mult, ALU.mult)
                nc.vector.tensor_scalar(t.sd[:, :, :], t.sd[:, :, :], rtop[:, 1:2], W_SCALE, ALU.mult, ALU.mult)
                link(nc.vector.tensor_scalar(t.y_out[:, :], topall[:, 0:1], topall[:, 1:2], None, ALU.mult))
                nc.vector.tensor_scalar(t.y_out[:, :], t.y_out[:, :], 1.0 / (H_BOUND_SCALE * W_SCALE), None, ALU.mult)
                lo_parts(0)
                dve.wait_ge(s_b, 32)
                for k in range(KT):
                    for j, wt in enumerate((wq, wk)):
                        b = bqk[:, 1 - j, k:k + 1]
                        if k == 0:
                            link(nc.vector.tensor_scalar(sums[:, j, :], wt[:, k, :], b, None, ALU.mult))
                        else:
                            link(nc.vector.scalar_tensor_tensor(out=sums[:, j, :], in0=wt[:, k, :], scalar=b, in1=sums[:, j, :],
                                                                op0=ALU.mult, op1=ALU.add))
                link(nc.vector.tensor_tensor(prod[:, :], bqk[:, 0, :], bqk[:, 1, :], ALU.mult))
                nc.vector.reduce_sum(bsum[:, :], prod[:, :], axis=AX.X).then_inc(s_sums, 1)
                for n in range(XQ):
                    dve.wait_ge(s_x[n], 16)
                    for i in range(n * NT // XQ, (n + 1) * NT // XQ):
                        nc.vector.bn_stats(stats[:, i % 2, 0, :], y[:, i, 0:BANK])
                        link(nc.vector.bn_stats(stats[:, i % 2, 1, :], y[:, i, BANK:DIM]))
                        last = nc.vector.bn_aggr(t.mv[:, i, :], stats[:, i % 2, :, :].rearrange("p a b -> p (a b)"))
                link(last)
                rsqrt(nc, t.rstd[:, :], t.mv[:, :, 1], t.guess[:, :], t.var[:, :], link)
                nc.vector.tensor_scalar(t.rstd[:, :], t.rstd[:, :], X_SCALE, None, ALU.mult)
                lo_parts(1)
                for n, _, kind in first:
                    keep_lo(nc, dve, un, t, n, *gate_up_dest(un, 0, *kind), UNIT_BANK + n % 2)
                dve.wait_ge(s_rows, 1)
                nc.vector.tensor_copy(t.key_row[:, :].rearrange("p (h n) -> p h n", h=HALVES), ps[:, 0:2, :])
                nc.vector.tensor_copy(t.query_col[:, :], ps[:, 2, 0:KT])
                nc.vector.tensor_copy(t.bias_dot[:, :], ps[:, 2, KT:KT + 1])


def attend(nc, t, un):
    with ExitStack() as st:
        def sb(name, shape, dt):
            return st.enter_context(nc.sbuf_tensor(name, shape, dt))

        def sem(name):
            return st.enter_context(nc.semaphore(name + "_a"))

        ps, y, ident = t.ps, t.y, t.ident
        ctx_dram = t.ctx.rearrange("b (t p) d -> b p t d", p=P)
        keys = sb("keys", [P, 2, TB, DIM], F32)
        keysT = sb("keysT", [P, KT, SEQ], F32)
        xn = sb("xn", [P, TB, DIM], F32)
        xnT = sb("xnT", [P, 2, KT, SEQ], F16)
        RT = sb("RT", [P, KT, SEQ], F32)
        probs = sb("probs", [P, TB, SEQ], F32)
        probsT = sb("probsT", [P, TB, SEQ], F32)
        dump = sb("dump", [P, DIM], F32)
        dots = sb("dots", [P, 2, TB], F32)
        sums = sb("sums", [P, TB], F32)
        rsum = sb("rsum", [P, 2, TB], F32)
        mx, row, top, dif, neg = (sb(n, [P, TB], F32) for n in ("mx", "row", "top_s", "dif", "neg"))
        fresh = sb("fresh", [P, TB, DIM], F32)
        all_stats = sb("all_stats", [P, NT, 2, 6], F32)
        stats = sb("stats2", [P, TB, 2, 6], F32)
        s_keys = [sem("s_keys0"), sem("s_keys1")]
        s_xn, s_dot, s_t, s_xhi, s_xlo, s_kev, s_r, s_rev, s_scores, s_neg, s_probs = (
            sem(n) for n in ("s_xn", "s_dot", "s_t", "s_xhi", "s_xlo", "s_kev", "s_r", "s_rev", "s_scores", "s_neg", "s_probs"))
        s_pt, s_ptev, s_att, s_y, s_copied, s_stats, s_self = (
            sem(n) for n in ("s_pt", "s_ptev", "s_att", "s_y", "s_copied", "s_stats", "s_self"))
        HALVES = DIM // BANK
        XG = TB * HALVES
        ATT = TB * HALVES

        later = [unit_of(0, n - FIRST_UNITS) if n >= FIRST_UNITS else (n, 0, (n // 2, n % 2))
                 for n in range(EARLY_UNITS, EARLY_UNITS + P_RING)]

        def batches(eng_loop, step):
            step(0, 0)
            with eng_loop(0, (BATCH - 2) // 2) as j:
                step(2 * j + 1, 1)
                step(2 * j + 2, 0)
            step(BATCH - 1, 1)

        with nc.Block() as block:
            @block.sync
            def _(sp):
                def load(b, parity):
                    if not isinstance(b, int) or b >= 2:
                        sp.wait_ge(s_att, ATT * (b - 1))
                    sp.dma_start(keys[:, parity, :, :],
                                 ctx_dram[bass.ds(b, 1)].rearrange("o p t d -> p (o t) d")).then_inc(s_keys[parity], 16)

                load(0, 0)
                for u, chunk, kind in later:
                    load_unit(nc, sp, un, t, u, u % Q_RING, chunk, kind)
                load(1, 1)
                with nc.sync.Fori(0, (BATCH - 2) // 2) as j:
                    load(2 * j + 2, 0)
                    load(2 * j + 3, 1)

            @block.gpsimd
            def _(pool):
                for i in range(TB):
                    nc.gpsimd.memset(fresh[:, i, :], 0.0).then_inc(s_copied, 1)
                for u, chunk, kind in later:
                    scale_unit(nc, pool, un, t, u, u % P_RING, chunk, kind)

                def keep(b, parity):
                    for i in range(TB):
                        pool.wait_ge(s_y, ATT * b + HALVES * (i + 1))
                        nc.gpsimd.tensor_copy(y[:, bass.ds(TB * b + i, 1), :].rearrange("p o d -> p (o d)"),
                                              fresh[:, i, :]).then_inc(s_copied, 1)

                batches(nc.gpsimd.Fori, keep)

            @block.tensor
            def _(pe):
                def turn(bank, src):
                    for k in range(4):
                        last = nc.tensor.transpose(ps[:, bank, k * P:(k + 1) * P], src[:, k * P:(k + 1) * P], ident[:, :])
                    last.then_inc(s_t, 1)

                def turn_probs(b):
                    pe.wait_ge(s_probs, TB * (b + 1))
                    for k in range(TB):
                        for i in range(TB):
                            last = nc.tensor.transpose(ps[:, 4, (k * TB + i) * P:(k * TB + i + 1) * P],
                                                       probs[:, i, k * P:(k + 1) * P], ident[:, :])
                    last.then_inc(s_pt, 1)

                def finish(b, parity):
                    pe.wait_ge(s_ptev, b + 1)
                    for i in range(TB):
                        for h in range(HALVES):
                            n = i * HALVES + h
                            if n >= 2:
                                pe.wait_ge(s_y, ATT * b + n - 1)
                            for k in range(TB):
                                last = nc.tensor.matmul(ps[:, 6 + n % 2, :], probsT[:, k, i * P:(i + 1) * P],
                                                        keys[:, parity, k, h * BANK:(h + 1) * BANK],
                                                        start=k == 0, stop=k == TB - 1)
                            last.then_inc(s_att, 1)

                def step(b, parity):
                    first = isinstance(b, int) and b == 0
                    for g in range(XG):
                        if g % HALVES == 0:
                            pe.wait_ge(s_xn, TB * b + g // HALVES + 1)
                        if g < 2 and not first:
                            pe.wait_ge(s_kev, XG * b + g - 1)
                        elif g >= 2:
                            pe.wait_ge(s_xlo, XG * b + g - 1)
                        turn(g % 2, xn[:, g // HALVES, g % HALVES * BANK:(g % HALVES + 1) * BANK])
                    pe.wait_ge(s_keys[parity], 8 * (b + 2 - parity))
                    for g in range(XG):
                        if g < 2:
                            pe.wait_ge(s_xlo, XG * b + XG + g - 1)
                        else:
                            pe.wait_ge(s_kev, XG * b + g - 1)
                        turn(g % 2, keys[:, parity, g // HALVES, g % HALVES * BANK:(g % HALVES + 1) * BANK])
                    pe.wait_ge(s_xlo, XG * (b + 1))
                    for o in range(KT):
                        wait(pe, s_rev, KT * b + o - 1)
                        for k in range(KT):
                            for j, (a, c) in enumerate(PARTS):
                                last = nc.tensor.matmul(ps[:, 2 + o % 2, 0:SEQ], t.A[:, a, k, o * P:(o + 1) * P], xnT[:, c, k, :],
                                                        start=k == 0 and j == 0, stop=k == KT - 1 and j == len(PARTS) - 1)
                        last.then_inc(s_r, 1)
                        if o == KT // 2 - 1 and not first:
                            turn_probs(b - 1)
                    if not first:
                        finish(b - 1, 1 - parity)
                    pe.wait_ge(s_rev, KT * (b + 1))
                    pe.wait_ge(s_kev, XG * (b + 1))
                    for i in range(TB):
                        for k in range(KT):
                            last = nc.tensor.matmul(ps[:, 4 + i, 0:SEQ], RT[:, k, i * P:(i + 1) * P], keysT[:, k, :],
                                                    start=k == 0, stop=k == KT - 1)
                        last.then_inc(s_scores, 1)

                batches(nc.tensor.Fori, step)
                turn_probs(BATCH - 1)
                finish(BATCH - 1, 1)

            @block.scalar
            def _(act):
                def step(b, parity):
                    first = isinstance(b, int) and b == 0
                    for g in range(2 * XG):
                        i, h = g // HALVES % TB, g % HALVES
                        src = ps[:, g % 2, :].rearrange("p (k t) -> p k t", k=4)
                        act.wait_ge(s_t, 2 * XG * b + g + 1)
                        if g < XG:
                            nc.scalar.copy(xnT[:, 0, 4 * h:4 * h + 4, i * P:(i + 1) * P], src).then_inc(s_xhi, 1)
                        else:
                            nc.scalar.copy(keysT[:, 4 * h:4 * h + 4, i * P:(i + 1) * P], src).then_inc(s_kev, 1)
                    for o in range(KT):
                        act.wait_ge(s_r, KT * b + o + 1)
                        nc.scalar.activation(RT[:, o, :], ps[:, 2 + o % 2, 0:SEQ], ACT.Identity, scale=t.a_out[:, 0:1],
                                             bias=t.query_col[:, o:o + 1]).then_inc(s_rev, 1)
                        if o == KT // 2 - 1 and not first:
                            turned_probs(b - 1)
                        if first:
                            for n in range(o * P_RING, (o + 1) * P_RING):
                                u = EARLY_UNITS + n // OPS
                                look_up(nc, act, un, u, u % P_RING, u % Q_RING, 16 * (u // Q_RING + 1), u % 2 == 0, (n % OPS,))
                    for i in range(TB):
                        act.wait_ge(s_neg, TB * b + i + 1)
                        nc.scalar.activation(probs[:, i, :], ps[:, 4 + i, 0:SEQ], ACT.Exp, bias=neg[:, i:i + 1],
                                             scale=SCORE_SCALE, accum_out=sums[:, i:i + 1]).then_inc(s_probs, 1)

                def turned_probs(b):
                    act.wait_ge(s_pt, b + 1)
                    nc.scalar.copy(probsT[:, :, :].rearrange("p k t -> p (k t)"), ps[:, 4, :]).then_inc(s_ptev, 1)

                batches(nc.scalar.Fori, step)
                turned_probs(BATCH - 1)

            @block.vector
            def _(dve):
                LINKS = 5 * TB + 1
                seen = [0]

                def link(b, op):
                    seen[0] += 1
                    op.then_inc(s_self, 1)
                    dve.wait_ge(s_self, LINKS * b + seen[0])

                def normalise(b, parity):
                    for i in range(TB):
                        if not isinstance(b, int) or b >= 1:
                            dve.wait_ge(s_t, 2 * XG * (b - 1) + HALVES * (i + 1))
                        nt = TB * b + i
                        nc.vector.tensor_scalar(xn[:, i, :], y[:, bass.ds(nt, 1), :].rearrange("p o d -> p (o d)"),
                                                t.mv[:, bass.ds(nt, 1), 0], t.rstd[:, bass.ds(nt, 1)],
                                                ALU.subtract, ALU.mult).then_inc(s_xn, 1)
                    for i in range(TB):
                        dve.wait_ge(s_xn, TB * b + i + 1)
                        wait(dve, s_dot, TB * b + i)
                        nc.vector.tensor_tensor_reduce(out=dump[:, :], in0=xn[:, i, :], in1=t.key_row[:, :], scale=1.0, scalar=0.0,
                                                       op0=ALU.mult, op1=ALU.add,
                                                       accum_out=dots[:, parity, i:i + 1]).then_inc(s_dot, 1)

                def lo_parts(b):
                    for g in range(XG):
                        i, h = g // HALVES, g % HALVES
                        dve.wait_ge(s_xhi, XG * b + g + 1)
                        nc.vector.tensor_tensor(xnT[:, 1, 4 * h:4 * h + 4, i * P:(i + 1) * P],
                                                ps[:, g % 2, :].rearrange("p (k t) -> p k t", k=4),
                                                xnT[:, 0, 4 * h:4 * h + 4, i * P:(i + 1) * P], ALU.subtract).then_inc(s_xlo, 1)

                def softmax(b, parity):
                    seen[0] = 0
                    dve.wait_ge(s_dot, TB * (b + 1))
                    for i in range(TB):
                        dve.wait_ge(s_scores, TB * b + i + 1)
                        link(b, nc.vector.reduce_max(mx[:, i:i + 1], ps[:, 4 + i, 0:SEQ], AX.X))
                        link(b, nc.vector.scalar_tensor_tensor(out=row[:, i:i + 1], in0=dots[:, parity, i:i + 1], scalar=1.0 / X_SCALE,
                                                               in1=t.bias_dot[:, :], op0=ALU.mult, op1=ALU.add))
                        link(b, nc.vector.tensor_tensor(top[:, i:i + 1], mx[:, i:i + 1], row[:, i:i + 1], ALU.add))
                        link(b, nc.vector.tensor_tensor(dif[:, i:i + 1], row[:, i:i + 1], top[:, i:i + 1], ALU.subtract))
                        nc.vector.tensor_scalar(neg[:, i:i + 1], dif[:, i:i + 1], SCORE_SCALE, None, ALU.mult).then_inc(s_neg, 1)
                    for i in range(TB):
                        dve.wait_ge(s_probs, TB * b + i + 1)
                        link(b, nc.vector.reciprocal(rsum[:, parity, i:i + 1], sums[:, i:i + 1]))

                def residual(b, parity):
                    seen[0] = 5 * TB
                    for i in range(TB):
                        for h in range(HALVES):
                            n = i * HALVES + h
                            cols = slice(h * BANK, (h + 1) * BANK)
                            dve.wait_ge(s_att, ATT * b + n + 1)
                            if h == 0:
                                dve.wait_ge(s_copied, TB * b + i + 1)
                            nc.vector.scalar_tensor_tensor(out=fresh[:, i, cols], in0=ps[:, 6 + n % 2, :],
                                                           scalar=rsum[:, parity, i:i + 1],
                                                           in1=y[:, bass.ds(TB * b + i, 1), cols].rearrange("p o d -> p (o d)"),
                                                           op0=ALU.mult, op1=ALU.add).then_inc(s_y, 1)
                    for i in range(TB):
                        dve.wait_ge(s_y, ATT * b + HALVES * (i + 1))
                        for h in range(HALVES):
                            last = nc.vector.bn_stats(stats[:, i, h, :], fresh[:, i, h * BANK:(h + 1) * BANK])
                    link(b, last)
                    nc.vector.tensor_copy(all_stats[:, bass.ds(TB * b, TB), :, :], stats[:, :, :, :]).then_inc(s_stats, 1)

                def step(b, parity):
                    first = isinstance(b, int) and b == 0
                    if first:
                        normalise(0, 0)
                    lo_parts(b)
                    if not (isinstance(b, int) and b == BATCH - 1):
                        normalise(b + 1, 1 - parity)
                    if first:
                        for u, _, _ in later:
                            for _ in factors(nc, dve, un, u, u % P_RING, u % 2 == 0):
                                pass
                    else:
                        residual(b - 1, 1 - parity)
                    softmax(b, parity)

                batches(nc.vector.Fori, step)
                residual(BATCH - 1, 1)
                total = [LINKS * BATCH]

                def link_after(op):
                    total[0] += 1
                    op.then_inc(s_self, 1)
                    dve.wait_ge(s_self, total[0])

                dve.wait_ge(s_stats, BATCH)
                for i in range(NT):
                    last = nc.vector.bn_aggr(t.mv[:, i, :], all_stats[:, i, :, :].rearrange("p a b -> p (a b)"))
                link_after(last)
                rsqrt(nc, t.rstd[:, :], t.mv[:, :, 1], t.guess[:, :], t.var[:, :], link_after)
                nc.vector.tensor_scalar(t.rstd[:, :], t.rstd[:, :], X_SCALE, None, ALU.mult)


def feed_forward(nc, t, un):
    with ExitStack() as st:
        def sb(name, shape, dt):
            return st.enter_context(nc.sbuf_tensor(name, shape, dt))

        def sem(name):
            return st.enter_context(nc.semaphore(name + "_f"))

        y, ps = t.y, t.ps
        xT = sb("xT", [P, 2, KT, TOK], F16)
        wd = sb("wd", [P, 3, 2, DIM], F16)
        h = sb("h", [P, 3, 2, TOK], F16)
        act_buf = sb("act_buf", [P, 2, BANK], F32)
        gate_now = sb("gate_now", [P, 2], F32)
        xn = h[:, 2, :, :].rearrange("p a b -> p (a b)").bitcast(F32).rearrange("p (i d) -> p i d", i=2)
        names = ("s_xn", "s_xt", "s_xhi", "s_xlo", "s_g", "s_u", "s_silu", "s_h", "s_hhi", "s_hlo", "s_down", "s_y", "s_out", "s_gate")
        s_xn, s_xt, s_xhi, s_xlo, s_g, s_u, s_silu, s_h, s_hhi, s_hlo, s_down, s_y, s_out, s_gate = (sem(n) for n in names)
        HALVES = DIM // BANK
        OUT = NT * HALVES
        XG = HALVES * NT // NBLK

        def weights_of(chunk_odd, down_parity, kind):
            mat, half = kind
            if mat < 2:
                return gate_up_dest(un, chunk_odd, mat, half)
            return [wd[:, slot_of(chunk_odd, down_parity), part, half * BANK:(half + 1) * BANK] for part in range(2)]

        def dest(p_parity, e):
            if e < 4:
                return weights_of(1, 0, (e // 2, e % 2))
            if e < 6:
                return weights_of(0, p_parity, (2, e - 4))
            if e < 10:
                return weights_of(0, 0, ((e - 6) // 2, e % 2))
            return weights_of(1, 0, (2, e - 10))

        def ahead(p, e):
            return (p, e + LEAD) if e + LEAD < EVENTS else (p + 1, e + LEAD - EVENTS)

        def exists(p, e):
            if isinstance(p, int) and p >= PERIODS:
                return False
            return has_unit(p, e)

        def count(p, e):
            u = FIRST_UNITS + EVENTS * p + e
            return u - 4 if isinstance(p, int) and p == PERIODS - 1 and e >= 10 else u

        def periods(eng_loop, period):
            period(0, 0)
            with eng_loop(0, (PERIODS - 2) // 2) as j:
                period(2 * j + 1, 1)
                period(2 * j + 2, 0)
            period(PERIODS - 1, (PERIODS - 1) % 2)

        def slot_number(u, e):
            return u if isinstance(u, int) else FIRST_UNITS + e

        def x_part(n, part):
            i, half = n // HALVES, n % HALVES
            return xT[:, part, 4 * half:4 * half + 4, i * P:(i + 1) * P]

        def next_x(p, e):
            return range((e + 1) * XG, (e + 2) * XG) if isinstance(p, int) and p == 0 and e < NBLK - 1 else ()

        with nc.Block() as block:
            @block.sync
            def _(sp):
                def load(u, ring, pair, chunk, kind):
                    if kind != (2, 0):
                        sp.wait_ge(un.s_act, OPS * (u + pair - Q_RING + 1))
                    load_unit(nc, sp, un, t, u, ring, chunk, kind)

                def period(p, parity):
                    for e in range(EVENTS):
                        if exists(p, e) and (e >= LEAD or not (isinstance(p, int) and p == 0)):
                            _, chunk, kind = unit_of(p, e)
                            u = count(p, e)
                            if not exists(p, e - 1) and kind == (2, 0):
                                sp.wait_ge(un.s_act, OPS * (u - Q_RING + 1))
                            load(u, slot_number(u, e) % Q_RING, e in (3, 9), chunk, kind)

                periods(nc.sync.Fori, period)
                for n in range(4):
                    sp.wait_ge(s_y, OUT * (PERIODS - 1) + (n + 1) * OUT // 4)
                    sp.dma_start(t.out_t[:, 4 * n:4 * n + 4, :], y[:, 4 * n:4 * n + 4, :]).then_inc(s_out, 16)
                sp.wait_ge(s_out, 64)

            @block.gpsimd
            def _(pool):
                def hidden_lo(p, parity, e):
                    odd, n = GU_EVENT[e]
                    b = NBLK * (2 * p + odd) + n
                    pool.wait_ge(s_hhi, b + 1)
                    cols = slice(n * BANK, (n + 1) * BANK)
                    s = slot_of(odd, parity)
                    nc.gpsimd.tensor_tensor(h[:, s, 1, cols], act_buf[:, n % 2, :], h[:, s, 0, cols], ALU.subtract).then_inc(s_hlo, 1)

                def period(p, parity):
                    for e in range(EVENTS):
                        p2, e2 = ahead(p, e)
                        if exists(p2, e2):
                            _, chunk, kind = unit_of(p2, e2)
                            u = count(p2, e2)
                            scale_unit(nc, pool, un, t, u, slot_number(u, e2) % P_RING, chunk, kind)
                        if e in GU_EVENT:
                            hidden_lo(p, parity, e)

                periods(nc.gpsimd.Fori, period)

            @block.scalar
            def _(act):
                def x_hi(n):
                    act.wait_ge(s_xt, n + 1)
                    nc.scalar.copy(x_part(n, 0), ps[:, 6 + n % 2, :].rearrange("p (k t) -> p k t", k=4)).then_inc(s_xhi, 1)

                def unit_args(p, e):
                    u = count(p, e)
                    k = slot_number(u, e)
                    q_count = 16 * (k // Q_RING + 1)
                    if not isinstance(u, int):
                        q_count = q_count + 16 * (EVENTS // Q_RING) * p
                    return u, k % P_RING, k % Q_RING, q_count, e % 2 == 0

                def weights_hi(p, parity, e):
                    keep_hi(nc, act, un, t, count(p, e), dest(parity, e)[0], e % 2)

                def silu(p, e):
                    odd, n = GU_EVENT[e]
                    b = NBLK * (2 * p + odd) + n
                    act.wait_ge(s_g, b + 1)
                    wait(act, s_hlo, b - 1)
                    if e == 0:
                        act.wait_ge(s_gate, p + 1)
                    nc.scalar.activation(act_buf[:, n % 2, :], ps[:, 2 + n % 2, :], ACT.Silu,
                                         scale=gate_now[:, odd:odd + 1]).then_inc(s_silu, 1)

                def hidden_hi(p, parity, e):
                    odd, n = GU_EVENT[e]
                    act.wait_ge(s_h, NBLK * (2 * p + odd) + n + 1)
                    nc.scalar.copy(h[:, slot_of(odd, parity), 0, n * BANK:(n + 1) * BANK], act_buf[:, n % 2, :]).then_inc(s_hhi, 1)

                def period(p, parity):
                    for e in range(EVENTS):
                        p2, e2 = ahead(p, e)
                        args = unit_args(p2, e2) if exists(p2, e2) else None
                        groups = next_x(p, e)
                        for i in range(OPS):
                            if i == OPS // 2 and e in GU_EVENT:
                                silu(p, e)
                            if args:
                                look_up(nc, act, un, *args, (i,))
                            if groups:
                                x_hi(groups[i])
                        if e in GU_EVENT:
                            hidden_hi(p, parity, e)
                        if exists(p, e):
                            weights_hi(p, parity, e)

                for u in range(EARLY_UNITS, FIRST_UNITS):
                    keep_hi(nc, act, un, t, u, gate_up_dest(un, 0, u // 2, u % 2)[0], u % 2)
                for n in range(XG):
                    x_hi(n)
                periods(nc.scalar.Fori, period)

            @block.vector
            def _(dve):
                def norm(i):
                    wait(dve, s_xt, HALVES * (i - 1))
                    nc.vector.tensor_scalar(xn[:, i % 2, :], y[:, i, :], t.mv[:, i, 0:1], t.rstd[:, i:i + 1],
                                            ALU.subtract, ALU.mult).then_inc(s_xn, 1)

                def x_lo(n):
                    dve.wait_ge(s_xhi, n + 1)
                    nc.vector.tensor_tensor(x_part(n, 1), ps[:, 6 + n % 2, :].rearrange("p (k t) -> p k t", k=4),
                                            x_part(n, 0), ALU.subtract).then_inc(s_xlo, 1)

                def weights_lo(p, parity, e):
                    keep_lo(nc, dve, un, t, count(p, e), *dest(parity, e), e % 2)

                def hidden(p, e):
                    odd, n = GU_EVENT[e]
                    b = NBLK * (2 * p + odd) + n
                    dve.wait_ge(s_u, b + 1)
                    dve.wait_ge(s_silu, b + 1)
                    nc.vector.scalar_tensor_tensor(out=act_buf[:, n % 2, :], in0=ps[:, 4 + n % 2, :],
                                                   scalar=t.up_out[:, bass.ds(2 * p + odd, 1)], in1=act_buf[:, n % 2, :],
                                                   op0=ALU.mult, op1=ALU.mult).then_inc(s_h, 1)

                def add_down(p, n):
                    i, hh = n // HALVES, n % HALVES
                    cols = slice(hh * BANK, (hh + 1) * BANK)
                    dve.wait_ge(s_down, OUT * p + n + 1)
                    nc.vector.scalar_tensor_tensor(out=y[:, i, cols], in0=ps[:, 6 + n % 2, :], scalar=t.y_out[:, 0:1],
                                                   in1=y[:, i, cols], op0=ALU.mult, op1=ALU.add).then_inc(s_y, 1)

                def period(p, parity):
                    wait(dve, s_silu, 2 * NBLK * p)
                    nc.vector.tensor_copy(gate_now[:, :], t.gate_out[:, bass.ds(2 * p, 2)]).then_inc(s_gate, 1)
                    for e in range(EVENTS):
                        p2, e2 = ahead(p, e)
                        todo = iter(())
                        if exists(p2, e2):
                            u = count(p2, e2)
                            todo = factors(nc, dve, un, u, slot_number(u, e2) % P_RING, e2 % 2 == 0)
                        for n in next_x(p, e):
                            if n % HALVES == 0 and n // HALVES + 1 < NT:
                                norm(n // HALVES + 1)
                            x_lo(n)
                            next(todo, None)
                        if e in DOWN_EVENT and not (isinstance(p, int) and p == 0):
                            for n in range(OUT // 4):
                                add_down(p - 1, DOWN_EVENT[e] * OUT // 4 + n)
                                next(todo, None)
                        for _ in todo:
                            pass
                        if e in GU_EVENT:
                            hidden(p, e)
                        if exists(p, e):
                            weights_lo(p, parity, e)

                norm(0)
                for u in range(EARLY_UNITS, FIRST_UNITS):
                    keep_lo(nc, dve, un, t, u, *gate_up_dest(un, 0, u // 2, u % 2), u % 2)
                for n in range(XG):
                    if n % HALVES == 0:
                        norm(n // HALVES + 1)
                    x_lo(n)
                periods(nc.vector.Fori, period)
                for n in range(OUT):
                    add_down(PERIODS - 1, n)

            @block.tensor
            def _(pe):
                def turn(u, slot, bank):
                    pe.wait_ge(un.s_wlo, u - 1)
                    turn_unit(nc, pe, un, t, u, slot, bank)

                def turn_x(n):
                    pe.wait_ge(s_xn, n // HALVES + 1)
                    wait(pe, s_xlo, n - 1)
                    for k in range(4):
                        src = xn[:, n // HALVES % 2, (n % HALVES * 4 + k) * P:(n % HALVES * 4 + k + 1) * P]
                        last = nc.tensor.transpose(ps[:, 6 + n % 2, k * P:(k + 1) * P], src, t.ident[:, :])
                    last.then_inc(s_xt, 1)

                def gate_up(p, e):
                    odd, n = GU_EVENT[e]
                    b = NBLK * (2 * p + odd) + n
                    wait(pe, s_h, b - 1)
                    groups = iter(next_x(p, e))
                    for mat, done in ((0, s_g), (1, s_u)):
                        for k in range(KT):
                            for j, (a, c) in enumerate(PARTS):
                                last = nc.tensor.matmul(ps[:, 2 + 2 * mat + n % 2, :], un.wgu[:, odd, mat, a, k, :],
                                                        xT[:, c, k, n * BANK:(n + 1) * BANK],
                                                        start=k == 0 and j == 0, stop=k == KT - 1 and j == 2)
                            if k % 2:
                                for group in groups:
                                    turn_x(group)
                                    break
                        last.then_inc(done, 1)

                def down(p, parity, n):
                    i, hh = n // HALVES, n % HALVES
                    if n >= 2:
                        pe.wait_ge(s_y, OUT * p + n - 1)
                    todo = [(s, a, c) for s in (slot_of(0, parity), slot_of(1, parity)) for a, c in PARTS]
                    for m, (s, a, c) in enumerate(todo):
                        last = nc.tensor.matmul(ps[:, 6 + n % 2, :], h[:, s, a, i * P:(i + 1) * P],
                                                wd[:, s, c, hh * BANK:(hh + 1) * BANK], start=m == 0, stop=m == len(todo) - 1)
                    last.then_inc(s_down, 1)

                def down_ready(p):
                    pe.wait_ge(s_hlo, NBLK * (2 * p + 2))
                    pe.wait_ge(un.s_wlo, count(p, EVENTS - 1) + 1)

                def period(p, parity):
                    for e in range(EVENTS):
                        if e == 0:
                            pe.wait_ge(un.s_wlo, FIRST_UNITS + EVENTS * (p - 1) + 10 if not isinstance(p, int) or p else FIRST_UNITS)
                        if e == 8:
                            pe.wait_ge(un.s_wlo, FIRST_UNITS + EVENTS * p + 4)
                        if e < NBLK and isinstance(p, int) and p == 0:
                            pe.wait_ge(s_xlo, (e + 1) * XG)
                        if e in GU_EVENT:
                            gate_up(p, e)
                        elif not (isinstance(p, int) and p == 0):
                            if e == 4:
                                down_ready(p - 1)
                            for n in range(OUT // 4):
                                down(p - 1, 1 - parity, DOWN_EVENT[e] * OUT // 4 + n)
                        if exists(p, e):
                            u = count(p, e)
                            turn(u, slot_number(u, e) % P_RING, e % 2)

                for u in range(EARLY_UNITS, FIRST_UNITS):
                    turn(u, u % P_RING, u % 2)
                for n in range(XG):
                    turn_x(n)
                periods(nc.tensor.Fori, period)
                last_pair = PERIODS - 1
                down_ready(last_pair)
                for n in range(OUT):
                    down(last_pair, last_pair % 2, n)


_INS = ["x", "ctx_4096", "L0_xattn_Wq", "L0_xattn_bq", "L0_xattn_Wk", "L0_xattn_bk", "L0_ffn_gate_q",
        "L0_ffn_gate_absmax", "L0_ffn_up_q", "L0_ffn_up_absmax", "L0_ffn_down_q", "L0_ffn_down_absmax"]


def kernel(**inputs):
    import concourse.bacc as bacc
    from concourse.bass_utils import run_bass_kernel_spmd

    nc = bacc.Bacc("TRN2", target_bir_lowering=False, num_devices=1)
    arrays, args = {}, []
    for name in _INS:
        a = np.ascontiguousarray(inputs[name])
        arrays[f"in_{name}"] = a
        args.append(nc.dram_tensor(f"in_{name}", a.shape, mybir.dt.from_np(a.dtype), kind="ExternalInput").ap())
    args.append(nc.dram_tensor("out_0", (BATCH, SEQ, DIM), F32, kind="ExternalOutput").ap())
    xattn_ffn_kernel(nc, *args)
    r = run_bass_kernel_spmd(nc, [arrays], core_ids=[0])
    return r.results[0]["out_0"]
```

```python
from contextlib import ExitStack

import numpy as np

import concourse.bass as bass
from concourse import mybir

ALU = mybir.AluOpType
ACT = mybir.ActivationFunctionType
AX = mybir.AxisListType
F32 = mybir.dt.float32
F16 = mybir.dt.float16
BF16 = mybir.dt.bfloat16
I32 = mybir.dt.int32

P = 128
BANK = 512
BATCH, SEQ, DIM = 8, 256, 1024
HID = 3584
QBLOCK = 64
TOK = BATCH * SEQ
KT = DIM // P
NT = TOK // P
TB = SEQ // P
CH = HID // P
KB = DIM // QBLOCK
MB = HID // QBLOCK
EPS = 1e-5
SCORE_SCALE = float(DIM) ** -0.5

X_SCALE = 1024.0
W_SCALE = 1024.0
H_BOUND_SCALE = 2.0 ** -5
A_BOUND = 2.0 ** 15
W_BOUND = 2.0 ** 15
R_BOUND = 2.0 ** 15
K_BOUND = 2.0 ** 14
P_SCALE = 1024.0
TINY = 1e-15
RSQRT_SEED = 0x5F3759DF
NEWTON_STEPS = 3

ZERO_CODE = 7.0
FACTORS = [
    (0.16843146085739136, -2.5078866481781006, 0.005980083718895912),
    (0.16843146085739136, -1.8140839338302612, 0.1702844202518463),
    (0.16843146085739136, -2.2222657203674316, 0.07722912728786469),
    (0.16843144595623016, -0.31645941734313965, 0.07142763584852219),
    (0.16843146085739136, -0.7382349967956543, 0.15366360545158386),
    (0.16843147575855255, -1.310221791267395, 0.17072737216949463),
    (0.16843146085739136, -0.024128910154104233, 0.005195258650928736),
]
NF = len(FACTORS)
OPS = NF + 1

GU_EVENT = {0: (0, 0), 1: (0, 1), 2: (0, 2), 3: (0, 3), 8: (1, 0), 9: (1, 1), 10: (1, 2), 11: (1, 3)}
FIRST_GU_EVENT = {0: (0, 0), 1: (0, 1), 2: (0, 2), 3: (0, 3), 4: (1, 0), 6: (1, 1), 8: (1, 2), 10: (1, 3)}
DOWN_EVENT = {4: 0, 5: 1, 6: 2, 7: 3}
EVENTS = 12
PERIODS = CH // 2
FIRST_UNITS = 4
UNITS = 6 * CH
LEAD = 2
NBLK = TOK // BANK
Q_RING, P_RING = 3, 3
ROW_BANK, COL_BANK = 4, 3
EARLY_UNITS = 3


def unit_of(p, e):
    u = FIRST_UNITS + EVENTS * p + e
    if e < 4:
        return u, 2 * p + 1, (e // 2, e % 2)
    if e < 6:
        return u, 2 * p, (2, e - 4)
    if e < 10:
        return u, 2 * p + 2, ((e - 6) // 2, e % 2)
    return u, 2 * p + 1, (2, e - 10)


def block_of(p, e):
    return (FIRST_GU_EVENT if isinstance(p, int) and p == 0 else GU_EVENT).get(e)


def down_of(p, e):
    return None if isinstance(p, int) and p == 0 else DOWN_EVENT.get(e)


def has_unit(p, e):
    return not (isinstance(p, int) and p == PERIODS - 1 and 6 <= e < 10)


def slot_of(odd, parity):
    return 1 if odd else 2 * parity


def wait(eng, sem, count):
    if not isinstance(count, int) or count > 0:
        eng.wait_ge(sem, count)


PARTS = ((0, 0), (0, 1), (1, 0))


def rsqrt(nc, out, var, guess, tmp, link):
    yield link(nc.vector.tensor_scalar(tmp, var, EPS, None, ALU.add))
    yield link(nc.vector.tensor_single_scalar(guess.bitcast(I32), tmp.bitcast(I32), 1, ALU.logical_shift_right))
    yield link(nc.vector.tensor_scalar(out.bitcast(I32), guess.bitcast(I32), -1.0, float(RSQRT_SEED), ALU.mult, ALU.add))
    for _ in range(NEWTON_STEPS):
        yield link(nc.vector.tensor_tensor(guess, out, out, ALU.mult))
        yield link(nc.vector.tensor_tensor(guess, guess, tmp, ALU.mult))
        yield link(nc.vector.tensor_scalar(guess, guess, -0.5, 1.5, ALU.mult, ALU.add))
        yield link(nc.vector.tensor_tensor(out, out, guess, ALU.mult))
    yield link(nc.vector.tensor_scalar(out, out, X_SCALE, None, ALU.mult))


class Shared:
    pass


class Units:

    def __init__(self, nc, stack):
        def sb(name, shape, dt):
            return stack.enter_context(nc.sbuf_tensor(name, shape, dt))

        def sem(name):
            return stack.enter_context(nc.semaphore(name))

        self.q = sb("q", [P, Q_RING, BANK], I32)
        self.sq = sb("sq", [P, 2, BANK], F32)
        self.w = sb("w", [P, P_RING, BANK], F32)
        self.wgu = sb("wgu", [P, 2, 2, 2, KT, P], F16)
        self.s_q = [sem(f"s_q{i}") for i in range(Q_RING)]
        self.s_act = sem("s_act")
        self.s_scaled = sem("s_scaled")
        self.s_fac = sem("s_fac")
        self.s_turned = sem("s_turned")
        self.s_whi = sem("s_whi")
        self.s_wlo = sem("s_wlo")


def load_unit(nc, eng, un, t, u, ring, chunk, kind):
    mat, half = kind
    if mat < 2:
        src = (t.gate_q, t.up_q)[mat][bass.ds(chunk * P, P), half * BANK:(half + 1) * BANK]
        eng.dma_start(un.q[:, ring, :], src).then_inc(un.s_q[ring], 16)
    else:
        src = t.down_q.rearrange("(k p) (c m) -> p k c m", p=P, m=P)[:, 4 * half:4 * half + 4, bass.ds(chunk, 1), :]
        src = src.rearrange("p k o m -> p k (o m)")
        eng.dma_start(un.q[:, ring, :].rearrange("p (k m) -> p k m", k=4), src).then_inc(un.s_q[ring], 16)


def scale_unit(nc, pool, un, t, u, slot, chunk, kind):
    mat, half = kind
    pool.wait_ge(un.s_act, OPS * u + 1)
    if mat < 2:
        tile = un.w[:, slot, :].rearrange("p (b j) -> p b j", j=QBLOCK)
        s = (t.sg, t.su)[mat][:, bass.ds(chunk, 1), half * KB // 2:(half + 1) * KB // 2]
        s = s.rearrange("p o b -> p (o b)").rearrange("p (b j) -> p b j", j=1).broadcast_to([P, KB // 2, QBLOCK])
    else:
        tile = un.w[:, slot, :].rearrange("p (k b j) -> p k b j", k=4, j=QBLOCK)
        s = t.sd[:, 4 * half:4 * half + 4, bass.ds(chunk * 2, 2)]
        s = s.rearrange("p k (b j) -> p k b j", j=1).broadcast_to([P, 4, 2, QBLOCK])
    nc.gpsimd.tensor_tensor(tile, tile, s, ALU.mult).then_inc(un.s_scaled, 1)


def look_up(nc, act, un, u, slot, ring, q_count, even, ops):
    for i in ops:
        if i == 0:
            act.wait_ge(un.s_q[ring], q_count)
            wait(act, un.s_turned, u - P_RING + 1)
            nc.scalar.activation(un.w[:, slot, :], un.q[:, ring, :], ACT.Copy, bias=-ZERO_CODE).then_inc(un.s_act, 1)
        else:
            wait(act, un.s_fac, NF * u + i - 2)
            a, b, _ = FACTORS[i - 1]
            nc.scalar.activation(un.sq[:, (i - even) % 2, :], un.q[:, ring, :], ACT.Square, bias=b,
                                 scale=a).then_inc(un.s_act, 1)


def factors(nc, dve, un, u, slot, even):
    for i in range(NF):
        if i == 0:
            dve.wait_ge(un.s_scaled, u + 1)
        else:
            dve.wait_ge(un.s_fac, NF * u + i)
        dve.wait_ge(un.s_act, OPS * u + i + 2)
        nc.vector.scalar_tensor_tensor(out=un.w[:, slot, :], in0=un.sq[:, (i + 1 - even) % 2, :], scalar=FACTORS[i][2],
                                       in1=un.w[:, slot, :], op0=ALU.add, op1=ALU.mult).then_inc(un.s_fac, 1)
        yield


def turn_unit(nc, pe, un, t, u, slot, bank):
    pe.wait_ge(un.s_fac, NF * (u + 1))
    for k in range(4):
        last = nc.tensor.transpose(t.ps[:, bank, k * P:(k + 1) * P], un.w[:, slot, k * P:(k + 1) * P], t.ident[:, :])
    last.then_inc(un.s_turned, 1)


def keep_hi(nc, act, un, t, u, dst, bank):
    act.wait_ge(un.s_turned, u + 1)
    nc.scalar.copy(dst, t.ps[:, bank, :]).then_inc(un.s_whi, 1)


def keep_lo(nc, dve, un, t, u, hi, lo, bank):
    dve.wait_ge(un.s_whi, u + 1)
    nc.vector.tensor_tensor(lo, t.ps[:, bank, :], hi, ALU.subtract).then_inc(un.s_wlo, 1)


def gate_up_dest(un, odd, mat, half):
    return [un.wgu[:, odd, mat, part, 4 * half:4 * half + 4, :].rearrange("p k m -> p (k m)") for part in range(2)]


def xattn_ffn_kernel(nc, x, ctx, Wq, bq, Wk, bk, gate_q, gate_absmax, up_q, up_absmax, down_q, down_absmax, out):
    with ExitStack() as whole:
        def sb(name, shape, dt):
            return whole.enter_context(nc.sbuf_tensor(name, shape, dt))

        t = Shared()
        t.Wq, t.bq, t.Wk, t.bk = Wq, bq, Wk, bk
        t.gate_q, t.up_q, t.down_q = gate_q, up_q, down_q
        t.gate_absmax, t.up_absmax, t.down_absmax = gate_absmax, up_absmax, down_absmax
        t.x_t = x.rearrange("b (t p) d -> p (b t) d", p=P)
        t.out_t = out.rearrange("b (t p) d -> p (b t) d", p=P)
        t.ctx_t = ctx.rearrange("b (t p) d -> b p t d", p=P)
        t.y = sb("y", [P, NT, DIM], F32)
        t.xT = sb("xT", [P, NBLK, 2, KT, BANK], F16)
        t.ident = sb("ident", [P, P], F32)
        t.sg = sb("sg", [P, CH, KB], F32)
        t.su = sb("su", [P, CH, KB], F32)
        t.sd = sb("sd", [P, KT, MB], F32)
        t.gate_out = sb("gate_out", [P, CH], F32)
        t.up_out = sb("up_out", [P, CH], F32)
        t.y_out = sb("y_out", [P, 1], F32)
        t.mv = sb("mv", [P, NT, 2], F32)
        t.rstd = sb("rstd", [P, NT], F32)
        t.all_stats = sb("all_stats", [P, NT, 2, 6], F32)
        t.guess = sb("guess", [P, NT], F32)
        t.var = sb("var", [P, NT], F32)
        t.ps = whole.enter_context(nc.psum_tensor("ps", [P, 8, BANK], F32))
        un = Units(nc, whole)
        with ExitStack() as attn:
            def sba(name, shape, dt):
                return attn.enter_context(nc.sbuf_tensor(name, shape, dt))

            t.A = t.xT[:, 2:4].rearrange("p n a k t -> p (n a k t)").rearrange("p (a k d) -> p a k d", a=2, k=KT)
            t.a_in = sba("a_in", [P, 1], F32)
            t.a_out = sba("a_out", [P, 1], F32)
            t.key_row = sba("key_row", [P, DIM], F32)
            t.query_col = sba("query_col", [P, KT], F32)
            t.r_out = sba("r_out", [P, 1], F32)
            t.r_in = sba("r_in", [P, 1], F32)
            t.bias_dot = sba("bias_dot", [P, 1], F32)
            t.kmax = sba("kmax", [P, 1], F32)
            t.kall = sba("kall", [P, 1], F32)
            t.keys, t.xn = (t.xT[:, 0, part].rearrange("p k t -> p (k t)").bitcast(F32).rearrange("p (i d) -> p i d", i=TB)
                            for part in range(2))
            prepare(nc, t, un)
            attend(nc, t, un)
        feed_forward(nc, t, un)


def prepare(nc, t, un):
    with ExitStack() as st:
        def sb(name, shape, dt):
            return st.enter_context(nc.sbuf_tensor(name, shape, dt))

        def sem(name):
            return st.enter_context(nc.semaphore(name))

        ps, y = t.ps, t.y
        HALVES = DIM // BANK
        BANKS = [COL_BANK, *range(ROW_BANK, ROW_BANK + HALVES)]
        BANKS += [i for i in range(KT) if i not in BANKS]
        XQ = 4
        LATE_SUMS = 4
        wq = t.xT[:, 0:2].rearrange("p n a k t -> p (n a k t)").bitcast(F32).rearrange("p (k d) -> p k d", k=KT)
        wk = sb("wk", [P, KT, DIM], F32)
        bqk = sb("bqk", [P, 2, KT], F32)
        prod = sb("prod", [P, KT], F32)
        bsum = sb("bsum", [P, 1], F32)
        ones = sb("ones", [P, P], F32)
        dump = sb("dump_x", [P, DIM], BF16)
        xsum = sb("xsum", [P, NT], F32)
        xdev = sb("xdev", [P, NT], F32)
        minus_mean = sb("minus_mean", [P, NT], F32)
        w_in = sb("w_in", [P, 2], F32)
        Sg = sb("Sg", [P, CH], F32)
        Su = sb("Su", [P, CH], F32)
        Rs = sb("Rs", [P, CH], F32)
        wmax = sb("wmax", [P, 2, KT], F32)
        top = sb("top", [P, 5], F32)
        topall = sb("topall", [P, 5], F32)
        rtop = sb("rtop", [P, 4], F32)
        sums = un.wgu[:, 1, :, :, :, :].rearrange("p m a k c -> p (m a k c)").bitcast(F32).rearrange("p (m d) -> p m d", m=2)

        def wq16(k):
            place = un.sq[:, :, :].rearrange("p a b -> p (a b)") if k == 0 else wq[:, k - 1, :]
            return place.bitcast(F16).rearrange("p (a d) -> p a d", a=2)

        def wk16(k):
            place = un.q[:, 0, :] if k == 0 else wk[:, k - 1, BANK:DIM]
            return place.bitcast(F16).rearrange("p (a d) -> p a d", a=2)

        s_split_hi, s_split_lo, s_xsum, s_mean, s_xdev = (sem(n) for n in ("s_split_hi", "s_split_lo", "s_xsum", "s_mean", "s_xdev"))
        A_IN_2 = A_BOUND / (DIM * W_BOUND * W_BOUND)
        s_w = [sem(f"s_w{k}") for k in range(KT)]
        s_wk2 = [sem(f"s_wk2{k}") for k in range(KT)]
        s_x = [sem(f"s_x{k}") for k in range(XQ)]
        s_split_used, s_keys, s_kmax = (sem(n) for n in ("s_split_used", "s_keys", "s_kmax"))
        s_b, s_abs, s_id, s_scales, s_sums = (sem(n) for n in ("s_b", "s_abs", "s_id", "s_scales", "s_sums"))
        s_acc, s_ahi, s_alo, s_top, s_topall, s_ain, s_self = (
            sem(n) for n in ("s_acc", "s_ahi", "s_alo", "s_top", "s_topall", "s_ain", "s_self"))
        first = [(n, 0, (n // 2, n % 2)) for n in range(EARLY_UNITS)]

        with nc.Block() as block:
            @block.sync
            def _(sp):
                for k in range(KT):
                    rows = slice(k * P, (k + 1) * P)
                    sp.dma_start(wq[:, k, :], t.Wq[rows, :]).then_inc(s_w[k], 16)
                    sp.dma_start(wk[:, k, 0:BANK], t.Wk[rows, 0:BANK]).then_inc(s_w[k], 16)
                for k in range(KT):
                    sp.dma_start(wk[:, k, BANK:DIM], t.Wk[k * P:(k + 1) * P, BANK:DIM]).then_inc(s_wk2[k], 16)
                for n in range(XQ):
                    tiles = slice(n * NT // XQ, (n + 1) * NT // XQ)
                    sp.dma_start(y[:, tiles, :], t.x_t[:, tiles, :]).then_inc(s_x[n], 16)
                sp.wait_ge(s_split_used, 3)
                sp.dma_start(t.keys[:, :, :], t.ctx_t[0]).then_inc(s_keys, 16)

            @block.scalar
            def _(act):
                act.dma_start(t.sg[:, :, :], t.gate_absmax.rearrange("(c p b) -> p c b", p=P, b=KB)).then_inc(s_abs, 16)
                act.dma_start(t.su[:, :, :], t.up_absmax.rearrange("(c p b) -> p c b", p=P, b=KB)).then_inc(s_abs, 16)
                act.dma_start(t.sd[:, :, :], t.down_absmax.rearrange("(k p b) -> p k b", p=P, b=MB)).then_inc(s_abs, 16)
                act.dma_start(bqk[:, 0, :], t.bq.rearrange("(k p) -> p k", p=P),
                              allow_slow_non_contiguous=True).then_inc(s_b, 16)
                act.dma_start(bqk[:, 1, :], t.bk.rearrange("(k p) -> p k", p=P),
                              allow_slow_non_contiguous=True).then_inc(s_b, 16)
                for n, chunk, kind in first:
                    load_unit(nc, act, un, t, n, n % Q_RING, chunk, kind)
                for n, chunk, kind in first:
                    look_up(nc, act, un, n, n % P_RING, n % Q_RING, 16 * (n // Q_RING + 1), n % 2 == 0, range(OPS))

                def x_sum(i):
                    if i % (NT // XQ) == 0:
                        act.wait_ge(s_x[i * XQ // NT], 16)
                    wait(act, s_xsum, i)
                    nc.scalar.activation(dump[:, :], y[:, i, :], ACT.Identity, accum_out=xsum[:, i:i + 1]).then_inc(s_xsum, 1)

                def x_square(i):
                    act.wait_ge(*((s_xdev, i) if i else (s_mean, 1)))
                    nc.scalar.activation(dump[:, :], y[:, i, :], ACT.Square, bias=minus_mean[:, i:i + 1],
                                         accum_out=xdev[:, i:i + 1]).then_inc(s_xdev, 1)

                def hi_parts(h, scale):
                    for n, i in enumerate(BANKS):
                        act.wait_ge(s_acc, h * KT + n + 1)
                        nc.scalar.activation(t.A[:, 0, i, h * BANK:(h + 1) * BANK], ps[:, i, :], ACT.Copy,
                                             scale=scale).then_inc(s_ahi, 1)

                for i in range(NT - LATE_SUMS):
                    x_sum(i)
                act.wait_ge(s_ain, 1)
                for k in range(KT):
                    wait(act, s_split_lo, k)
                    nc.scalar.activation(wq16(k)[:, 0, :], wq[:, k, :], ACT.Copy, scale=w_in[:, 0:1])
                    nc.scalar.activation(wk16(k)[:, 0, :], wk[:, k, BANK:DIM], ACT.Copy, scale=w_in[:, 1:2]).then_inc(s_split_hi, 1)
                    if k == 0:
                        hi_parts(0, t.a_in[:, 0:1])
                    elif k < 3:
                        for i in range(NT - LATE_SUMS * (3 - k) // 2, NT - LATE_SUMS * (2 - k) // 2):
                            x_sum(i)
                    else:
                        for i in range(NT * (k - 3) // (KT - 3), NT * (k - 2) // (KT - 3)):
                            x_square(i)
                hi_parts(1, A_IN_2)

            @block.gpsimd
            def _(pool):
                nc.gpsimd.memset(t.ident[:, :], 0.0).then_inc(s_id, 1)
                nc.gpsimd.memset(ones[:, :], 1.0).then_inc(s_id, 1)
                pool.wait_ge(s_id, 2)
                nc.gpsimd.affine_select(out=t.ident[:, :], in_=t.ident[:, :], compare_op=ALU.not_equal, fill=1.0, base=0,
                                        pattern=[[-1, P]], channel_multiplier=1).then_inc(s_id, 1)
                pool.wait_ge(s_top, 1)
                nc.gpsimd.partition_all_reduce(topall[:, 0:2], top[:, 0:2], P, bass.bass_isa.ReduceOp.max).then_inc(s_topall, 1)
                pool.wait_ge(s_scales, 1)
                for n, chunk, kind in first:
                    scale_unit(nc, pool, un, t, n, n % P_RING, chunk, kind)
                pool.wait_ge(s_top, 2)
                nc.gpsimd.partition_all_reduce(topall[:, 2:5], top[:, 2:5], P, bass.bass_isa.ReduceOp.max).then_inc(s_topall, 1)
                pool.wait_ge(s_kmax, 1)
                nc.gpsimd.partition_all_reduce(t.kall[:, :], t.kmax[:, :], P, bass.bass_isa.ReduceOp.max)

            @block.tensor
            def _(pe):
                for k in range(KT):
                    pe.wait_ge(s_w[k], 32)
                    for i in BANKS:
                        last = nc.tensor.matmul(ps[:, i, :], wq[:, k, i * P:(i + 1) * P], wk[:, k, 0:BANK], start=k == 0, stop=k == KT - 1)
                        if k == KT - 1:
                            last.then_inc(s_acc, 1)
                for k in range(KT):
                    pe.wait_ge(s_split_lo, k + 1)
                    for n, i in enumerate(BANKS):
                        if k == 0:
                            pe.wait_ge(s_alo, n + 1)
                        for j, (a, c) in enumerate(PARTS):
                            last = nc.tensor.matmul(ps[:, i, :], wq16(k)[:, a, i * P:(i + 1) * P], wk16(k)[:, c, :],
                                                    start=k == 0 and j == 0, stop=k == KT - 1 and j == len(PARTS) - 1)
                        if k == KT - 1:
                            last.then_inc(s_acc, 1)
                    if k < KT - 1:
                        last.then_inc(s_split_used, 1)
                pe.wait_ge(s_alo, KT + 1 + HALVES)
                pe.wait_ge(s_sums, 1)
                for h in range(HALVES):
                    nc.tensor.matmul(ps[:, ROW_BANK + h, :], ones[:, :], sums[:, 0, h * BANK:(h + 1) * BANK], start=True, stop=True)
                for i in range(KT):
                    nc.tensor.matmul(ps[:, COL_BANK, i:i + 1], sums[:, 1, i * P:(i + 1) * P], ones[:, 0:1], start=True, stop=True)
                nc.tensor.matmul(ps[:, COL_BANK, KT:KT + 1], ones[:, :], bsum[:, :], start=True, stop=True)

            @block.vector
            def _(dve):
                done = [0]

                def link(op):
                    done[0] += 1
                    op.then_inc(s_self, 1)
                    dve.wait_ge(s_self, done[0])

                def lo_parts(h, scale):
                    for n, i in enumerate(BANKS):
                        dve.wait_ge(s_ahi, h * KT + n + 1)
                        cols = slice(h * BANK, (h + 1) * BANK)
                        nc.vector.scalar_tensor_tensor(out=t.A[:, 1, i, cols], in0=ps[:, i, :], scalar=scale,
                                                       in1=t.A[:, 0, i, cols], op0=ALU.mult, op1=ALU.subtract).then_inc(s_alo, 1)

                def bias_sums(k):
                    for j, wt in enumerate((wq, wk)):
                        b = bqk[:, 1 - j, k:k + 1]
                        if k == 0:
                            link(nc.vector.tensor_scalar(sums[:, j, :], wt[:, k, :], b, None, ALU.mult))
                        else:
                            link(nc.vector.scalar_tensor_tensor(out=sums[:, j, :], in0=wt[:, k, :], scalar=b, in1=sums[:, j, :],
                                                                op0=ALU.mult, op1=ALU.add))

                dve.wait_ge(s_abs, 48)
                for n, (S, s) in enumerate(((Sg, t.sg), (Su, t.su))):
                    link(nc.vector.tensor_reduce(S[:, :], s[:, :, :], axis=AX.X, op=ALU.max, apply_absolute_value=True))
                    link(nc.vector.tensor_scalar(S[:, :], S[:, :], TINY, None, ALU.max))
                    link(nc.vector.reciprocal(Rs[:, :], S[:, :]))
                    link(nc.vector.tensor_scalar(Rs[:, :], Rs[:, :], W_SCALE, None, ALU.mult))
                    link(nc.vector.tensor_tensor(s[:, :, :], s[:, :, :],
                                                 Rs[:, :].rearrange("p (c o) -> p c o", o=1).broadcast_to([P, CH, KB]), ALU.mult))
                nc.vector.tensor_scalar(t.gate_out[:, :], Sg[:, :], 1.0 / (X_SCALE * W_SCALE), None,
                                        ALU.mult).then_inc(s_scales, 1)
                link(nc.vector.tensor_tensor(Rs[:, :], Sg[:, :], Su[:, :], ALU.mult))
                link(nc.vector.tensor_reduce(top[:, 0:1], Rs[:, :], axis=AX.X, op=ALU.max))
                link(nc.vector.tensor_reduce(top[:, 1:2], t.sd[:, :, :], axis=AX.XY, op=ALU.max, apply_absolute_value=True))
                nc.vector.tensor_scalar(top[:, 1:2], top[:, 1:2], TINY, None, ALU.max).then_inc(s_top, 1)
                for n, _, _ in first:
                    for _ in factors(nc, dve, un, n, n % P_RING, n % 2 == 0):
                        pass
                for k in range(KT):
                    dve.wait_ge(s_w[k], 32)
                    nc.vector.tensor_reduce(wmax[:, 0, k:k + 1], wq[:, k, :], axis=AX.X, op=ALU.max, apply_absolute_value=True)
                for k in range(KT):
                    dve.wait_ge(s_wk2[k], 16)
                    last = nc.vector.tensor_reduce(wmax[:, 1, k:k + 1], wk[:, k, :], axis=AX.X, op=ALU.max,
                                                   apply_absolute_value=True)
                link(last)
                link(nc.vector.tensor_reduce(top[:, 2:4], wmax[:, :, :], axis=AX.X, op=ALU.max))
                dve.wait_ge(s_b, 32)
                nc.vector.tensor_reduce(top[:, 4:5], bqk[:, 0, :], axis=AX.X, op=ALU.max, apply_absolute_value=True)
                nc.vector.tensor_scalar(top[:, 2:4], top[:, 2:4], TINY, None, ALU.max).then_inc(s_top, 1)
                bias_sums(0)
                dve.wait_ge(s_topall, 2)
                link(nc.vector.reciprocal(rtop[:, :], topall[:, 0:4]))
                nc.vector.tensor_scalar(w_in[:, :], rtop[:, 2:4], W_BOUND, None, ALU.mult)
                link(nc.vector.tensor_scalar(t.a_in[:, :], rtop[:, 2:3], rtop[:, 3:4], None, ALU.mult))
                nc.vector.tensor_scalar(t.a_in[:, :], t.a_in[:, :], A_BOUND / DIM, None, ALU.mult).then_inc(s_ain, 1)
                link(nc.vector.tensor_scalar(t.a_out[:, :], topall[:, 2:3], topall[:, 3:4], None, ALU.mult))
                link(nc.vector.tensor_scalar(t.r_out[:, :], topall[:, 2:3], DIM, topall[:, 4:5], ALU.mult, ALU.add))
                link(nc.vector.tensor_scalar(t.r_out[:, :], t.r_out[:, :], topall[:, 3:4], DIM / R_BOUND, ALU.mult, ALU.mult))
                link(nc.vector.reciprocal(t.r_in[:, :], t.r_out[:, :]))
                nc.vector.tensor_scalar(t.a_out[:, :], t.a_out[:, :], t.r_in[:, :], DIM / (A_BOUND * X_SCALE), ALU.mult, ALU.mult)
                nc.vector.tensor_scalar(t.up_out[:, :], Su[:, :], rtop[:, 0:1], H_BOUND_SCALE / (X_SCALE * W_SCALE),
                                        ALU.mult, ALU.mult)
                nc.vector.tensor_scalar(t.sd[:, :, :], t.sd[:, :, :], rtop[:, 1:2], W_SCALE, ALU.mult, ALU.mult)
                link(nc.vector.tensor_scalar(t.y_out[:, :], topall[:, 0:1], topall[:, 1:2], None, ALU.mult))
                nc.vector.tensor_scalar(t.y_out[:, :], t.y_out[:, :], 1.0 / (H_BOUND_SCALE * W_SCALE), None, ALU.mult)
                bias_sums(1)
                for k in range(KT):
                    dve.wait_ge(s_split_hi, k + 1)
                    for j, (wt, split) in enumerate(((wq[:, k, :], wq16(k)), (wk[:, k, BANK:DIM], wk16(k)))):
                        last = nc.vector.scalar_tensor_tensor(out=split[:, 1, :], in0=wt, scalar=w_in[:, j:j + 1], in1=split[:, 0, :],
                                                              op0=ALU.mult, op1=ALU.subtract)
                    last.then_inc(s_split_lo, 1)
                    if k == 0:
                        lo_parts(0, t.a_in[:, 0:1])
                    if k == 2:
                        dve.wait_ge(s_xsum, NT)
                        nc.vector.tensor_scalar(t.mv[:, :, 0], xsum[:, :], 1.0 / DIM, None, ALU.mult)
                        nc.vector.tensor_scalar(minus_mean[:, :], xsum[:, :], -1.0 / DIM, None, ALU.mult).then_inc(s_mean, 1)
                    if 1 <= k < KT - 1:
                        bias_sums(k + 1)
                link(nc.vector.tensor_tensor(prod[:, :], bqk[:, 0, :], bqk[:, 1, :], ALU.mult))
                nc.vector.reduce_sum(bsum[:, :], prod[:, :], axis=AX.X).then_inc(s_sums, 1)
                dve.wait_ge(s_keys, 16)
                nc.vector.tensor_reduce(t.kmax[:, :], t.keys[:, :, :], axis=AX.XY, op=ALU.max,
                                        apply_absolute_value=True).then_inc(s_kmax, 1)
                dve.wait_ge(s_xdev, NT)
                link(nc.vector.tensor_scalar(t.mv[:, :, 1], xdev[:, :], 1.0 / DIM, None, ALU.mult))
                for _ in rsqrt(nc, t.rstd[:, :], t.mv[:, :, 1], t.guess[:, :], t.var[:, :], link):
                    pass
                lo_parts(1, A_IN_2)
                dve.wait_ge(s_split_used, 5)
                for i in range(TB):
                    nc.vector.tensor_scalar(t.xn[:, i, :], y[:, i, :], t.mv[:, i, 0:1], t.rstd[:, i:i + 1], ALU.subtract, ALU.mult)


def attend(nc, t, un):
    with ExitStack() as st:
        def sb(name, shape, dt):
            return st.enter_context(nc.sbuf_tensor(name, shape, dt))

        def sem(name):
            return st.enter_context(nc.semaphore(name + "_a"))

        ps, y, ident = t.ps, t.y, t.ident
        keys, xn, kmax, kall = t.keys, t.xn, t.kmax, t.kall
        keys16 = t.xT[:, 1].rearrange("p a k t -> p (a k t)").rearrange("p (b a i d) -> p b a i d", b=2, a=2, i=TB)
        keysT = sb("keysT", [P, 2, KT, SEQ], F16)
        yn = sb("yn", [P, 2, DIM], F32)
        xnT = un.wgu[:, 1, :, :, :, :].rearrange("p m a k c -> p (m a k c)").rearrange("p (a k t) -> p a k t", a=2, k=KT)
        R_RING = 4
        R32 = sb("R32", [P, R_RING, SEQ], F32)
        RT = sb("RT", [P, 2, KT, SEQ], F16)
        probs = sb("probs", [P, TB, SEQ], F32)
        probsT = sb("probsT", [P, 2, TB, SEQ], F16)
        rk, k_in, spare = (sb(n, [P, 1], F32) for n in ("rk", "k_in", "spare"))
        score_out, exp_out, att_out = (sb(n, [P, 2], F32) for n in ("score_out", "exp_out", "att_out"))
        dump = sb("dump", [P, DIM], F32)
        dots = sb("dots", [P, 2, TB], F32)
        sums = sb("sums", [P, TB], F32)
        rsum = sb("rsum", [P, 2, TB], F32)
        mx, row, top, neg = (sb(n, [P, TB], F32) for n in ("mx", "row", "top_s", "neg"))
        stats = sb("stats2", [P, TB, 2, 6], F32)
        s_keys = sem("s_keys")
        s_kmax, s_kall, s_kin, s_khi, s_klo, s_ktlo, s_rlo, s_ptlo, s_out = (
            sem(n) for n in ("s_kmax", "s_kall", "s_kin", "s_khi", "s_klo", "s_ktlo", "s_rlo", "s_ptlo", "s_attout"))
        s_xn, s_dot, s_t, s_xhi, s_xlo, s_kev, s_r, s_rev, s_scores, s_neg, s_probs = (
            sem(n) for n in ("s_xn", "s_dot", "s_t", "s_xhi", "s_xlo", "s_kev", "s_r", "s_rev", "s_scores", "s_neg", "s_probs"))
        s_pt, s_ptev, s_att, s_y, s_bn, s_stats, s_ln, s_bias, s_self = (
            sem(n) for n in ("s_pt", "s_ptev", "s_att", "s_y", "s_bn", "s_stats", "s_ln", "s_bias", "s_self"))
        HALVES = DIM // BANK
        XG = TB * HALVES
        ATT = TB * HALVES
        SCALE_AT = range(2, 2 + 2 * TB)
        PROBS_AT = 1
        KEYS_AT = range(4, 4 + XG)
        Y_GROUPS = HALVES * NT // NBLK
        Y_BETWEEN = 2
        X_FINISH = (1, 3)
        X_AT = (4, 2)
        UNIT_BANK = 6

        def unit_dest(u):
            return gate_up_dest(un, 0, u // 2, u % 2)

        def unit_bank(u):
            return UNIT_BANK + u % 2


        later = [unit_of(0, n - FIRST_UNITS) if n >= FIRST_UNITS else (n, 0, (n // 2, n % 2))
                 for n in range(EARLY_UNITS, FIRST_UNITS + LEAD)]
        LATER = {0: later[:2], BATCH - 1: later[2:]}
        FACTORS_AT = {0: (NF, 1, 2, 2), BATCH - 1: (3, 1, 1, 1)}

        def x_group(b, g):
            i, h = g // HALVES, g % HALVES
            cols = slice(h * BANK, (h + 1) * BANK)
            if isinstance(b, int) and b == BATCH:
                return yn[:, i % 2, cols], [t.xT[:, 0, part, 4 * h:4 * h + 4, i * P:(i + 1) * P] for part in range(2)]
            return xn[:, i, cols], [xnT[:, part, 4 * h:4 * h + 4, i * P:(i + 1) * P] for part in range(2)]

        def batches(eng_loop, step):
            step(0, 0)
            with eng_loop(0, (BATCH - 2) // 2) as j:
                step(2 * j + 1, 1)
                step(2 * j + 2, 0)
            step(BATCH - 1, 1)

        with nc.Block() as block:
            @block.sync
            def _(sp):
                def load(b, parity):
                    sp.wait_ge(s_ktlo, XG * b)
                    sp.dma_start(keys[:, :, :], t.ctx_t[bass.ds(b, 1)].rearrange("o p t d -> p (o t) d")).then_inc(s_keys, 16)

                for u, chunk, kind in later[:Q_RING]:
                    load_unit(nc, sp, un, t, u, u % Q_RING, chunk, kind)
                with nc.sync.Fori(0, (BATCH - 2) // 2) as j:
                    load(2 * j + 1, 1)
                    load(2 * j + 2, 0)
                for u, chunk, kind in later[Q_RING:]:
                    sp.wait_ge(un.s_act, OPS * (u - Q_RING + 1))
                    load_unit(nc, sp, un, t, u, u % Q_RING, chunk, kind)
                load(BATCH - 1, 1)

            @block.gpsimd
            def _(pool):
                def reduce_max(b):
                    pool.wait_ge(s_kmax, b)
                    nc.gpsimd.tensor_tensor(spare[:, :], kmax[:, :], kmax[:, :], ALU.subtract)
                    nc.gpsimd.partition_all_reduce(kall[:, :], kmax[:, :], P, bass.bass_isa.ReduceOp.max).then_inc(s_kall, 1)

                def step(b, parity):
                    first = isinstance(b, int) and b == 0
                    for o in range(KT):
                        pool.wait_ge(s_rev, KT * b + o + 1)
                        nc.gpsimd.tensor_tensor(RT[:, 1, o, :], R32[:, o % R_RING, :], RT[:, 0, o, :], ALU.subtract).then_inc(s_rlo, 1)
                        if o in SCALE_AT[1::2]:
                            i = (o - SCALE_AT[0]) // 2
                            pool.wait_ge(s_khi, TB * b + i + 1)
                            nc.gpsimd.tensor_tensor(keys16[:, parity, 1, i, :], keys[:, i, :], keys16[:, parity, 0, i, :],
                                                    ALU.subtract).then_inc(s_klo, 1)
                        units = LATER.get(b, ()) if isinstance(b, int) else ()
                        for n in range(o * len(units), (o + 1) * len(units)):
                            if n % OPS == 0:
                                u, chunk, kind = units[n // OPS]
                                scale_unit(nc, pool, un, t, u, u % P_RING, chunk, kind)
                    if not (isinstance(b, int) and b == BATCH - 1):
                        reduce_max(b + 1)

                batches(nc.gpsimd.Fori, step)

            @block.tensor
            def _(pe):
                def turn(bank, src):
                    for k in range(4):
                        last = nc.tensor.transpose(ps[:, bank, k * P:(k + 1) * P], src[:, k * P:(k + 1) * P], ident[:, :])
                    last.then_inc(s_t, 1)

                def turn_probs(b):
                    pe.wait_ge(s_probs, TB * (b + 1))
                    for k in range(TB):
                        for i in range(TB):
                            last = nc.tensor.transpose(ps[:, 4, (k * TB + i) * P:(k * TB + i + 1) * P],
                                                       probs[:, i, k * P:(k + 1) * P], ident[:, :])
                    last.then_inc(s_pt, 1)

                def finish(b, parity):
                    pe.wait_ge(s_ptlo, b + 1)
                    pe.wait_ge(s_klo, TB * (b + 1))
                    for i in range(TB):
                        for h in range(HALVES):
                            n = i * HALVES + h
                            if n >= 2:
                                pe.wait_ge(s_y, ATT * b + n - 1)
                            todo = [(k, a, c) for k in range(TB) for a, c in PARTS]
                            for m, (k, a, c) in enumerate(todo):
                                last = nc.tensor.matmul(ps[:, 6 + n % 2, :], probsT[:, a, k, i * P:(i + 1) * P],
                                                        keys16[:, parity, c, k, h * BANK:(h + 1) * BANK],
                                                        start=m == 0, stop=m == len(todo) - 1)
                            last.then_inc(s_att, 1)
                            if isinstance(b, int) and b == BATCH - 1:
                                if XG + Y_BETWEEN + n < Y_GROUPS:
                                    turn_x(BATCH, XG + Y_BETWEEN + n)
                            elif n in X_FINISH:
                                turn_x(b + 2, X_FINISH.index(n))

                def turn_x(b, g):
                    if not isinstance(b, int) or b > 0:
                        pe.wait_ge(s_xn, TB * (b - 1) + g // HALVES + 1)
                    if g >= 2:
                        pe.wait_ge(s_xlo, XG * b + g - 1)
                    elif not isinstance(b, int) or b > 0:
                        pe.wait_ge(s_ktlo, XG * b + g - 1)
                    turn(g % 2, x_group(b, g)[0])

                def turn_keys(b, g):
                    if g % HALVES == 0:
                        pe.wait_ge(s_khi, TB * b + g // HALVES + 1)
                    if g < 2:
                        pe.wait_ge(s_xlo, XG * b + XG + g - 1)
                    else:
                        pe.wait_ge(s_ktlo, XG * b + g - 1)
                    turn(g % 2, keys[:, g // HALVES, g % HALVES * BANK:(g % HALVES + 1) * BANK])

                def step(b, parity):
                    first = isinstance(b, int) and b == 0
                    last_one = isinstance(b, int) and b == BATCH - 1
                    if last_one:
                        pe.wait_ge(s_y, ATT * (b - 1))
                        turn_unit(nc, pe, un, t, EARLY_UNITS, EARLY_UNITS % P_RING, unit_bank(EARLY_UNITS))
                    pe.wait_ge(s_xlo, XG * (b + 1))
                    for o in range(KT):
                        wait(pe, s_rev, KT * b + o - 1)
                        if first and o == 1:
                            pe.wait_ge(s_bias, 1)
                        for k in range(KT):
                            for j, (a, c) in enumerate(PARTS):
                                last = nc.tensor.matmul(ps[:, 2 + o % 2, 0:SEQ], t.A[:, a, k, o * P:(o + 1) * P], xnT[:, c, k, :],
                                                        start=k == 0 and j == 0, stop=k == KT - 1 and j == len(PARTS) - 1)
                        last.then_inc(s_r, 1)
                        if o == PROBS_AT and not first:
                            turn_probs(b - 1)
                        if o == PROBS_AT and first:
                            for u in range(2, EARLY_UNITS):
                                turn_early(u)
                        if o in KEYS_AT:
                            turn_keys(b, o - KEYS_AT[0])
                    if first:
                        for g in range(len(X_FINISH)):
                            turn_x(b + 1, g)
                    else:
                        if last_one:
                            pe.wait_ge(un.s_wlo, FIRST_UNITS)
                        finish(b - 1, 1 - parity)
                    pe.wait_ge(s_ktlo, XG * (b + 1))
                    for i in range(TB):
                        for k in range(KT):
                            if i == 0:
                                pe.wait_ge(s_rlo, KT * b + k + 1)
                            for j, (a, c) in enumerate(PARTS):
                                last = nc.tensor.matmul(ps[:, 4 + i, 0:SEQ], RT[:, a, k, i * P:(i + 1) * P], keysT[:, c, k, :],
                                                        start=k == 0 and j == 0, stop=k == KT - 1 and j == len(PARTS) - 1)
                            if k == X_AT[i]:
                                turn_x(b + 1, len(X_FINISH) + i)
                        last.then_inc(s_scores, 1)
                    if last_one:
                        for n in range(Y_BETWEEN):
                            turn_x(BATCH, XG + n)

                def turn_early(u):
                    wait(pe, un.s_wlo, u - 1)
                    turn_unit(nc, pe, un, t, u, u % P_RING, unit_bank(u))

                for g in range(XG):
                    if g >= 2:
                        turn_early(g - 2)
                    turn_x(0, g)
                batches(nc.tensor.Fori, step)
                turn_probs(BATCH - 1)
                finish(BATCH - 1, 1)

            @block.scalar
            def _(act):
                def x_hi(b, g):
                    act.wait_ge(s_t, 2 * XG * b + g + 1)
                    if isinstance(b, int) and b == BATCH and g == 0:
                        act.wait_ge(s_klo, TB * BATCH)
                    nc.scalar.copy(x_group(b, g)[1][0], ps[:, g % 2, :].rearrange("p (k t) -> p k t", k=4)).then_inc(s_xhi, 1)

                def step(b, parity):
                    first = isinstance(b, int) and b == 0
                    last_one = isinstance(b, int) and b == BATCH - 1
                    for o in range(KT):
                        act.wait_ge(s_r, KT * b + o + 1)
                        wait(act, s_rlo, KT * b + o - R_RING + 1)
                        nc.scalar.activation(R32[:, o % R_RING, :], ps[:, 2 + o % 2, 0:SEQ], ACT.Identity, scale=t.a_out[:, 0:1],
                                             bias=t.query_col[:, o:o + 1])
                        nc.scalar.activation(RT[:, 0, o, :], ps[:, 2 + o % 2, 0:SEQ], ACT.Identity, scale=t.a_out[:, 0:1],
                                             bias=t.query_col[:, o:o + 1]).then_inc(s_rev, 1)
                        if o in SCALE_AT:
                            i, hi = (o - SCALE_AT[0]) // 2, (o - SCALE_AT[0]) % 2 == 0
                            if hi:
                                act.wait_ge(s_kin, b + 1)
                                nc.scalar.activation(keys16[:, parity, 0, i, :], keys[:, i, :], ACT.Copy, scale=k_in[:, 0:1])
                            else:
                                nc.scalar.activation(keys[:, i, :], keys[:, i, :], ACT.Copy, scale=k_in[:, 0:1]).then_inc(s_khi, 1)
                        if o == PROBS_AT and not first:
                            turned_probs(b - 1)
                        if o == PROBS_AT and first:
                            for u in range(2, EARLY_UNITS):
                                keep_hi(nc, act, un, t, u, unit_dest(u)[0], unit_bank(u))
                        if o in KEYS_AT:
                            g = o - KEYS_AT[0]
                            i, h = g // HALVES, g % HALVES
                            act.wait_ge(s_t, 2 * XG * b + XG + g + 1)
                            nc.scalar.copy(keysT[:, 0, 4 * h:4 * h + 4, i * P:(i + 1) * P],
                                           ps[:, g % 2, :].rearrange("p (k t) -> p k t", k=4)).then_inc(s_kev, 1)
                        units = LATER.get(b, ()) if isinstance(b, int) else ()
                        for n in range(o * len(units), (o + 1) * len(units)):
                            u = units[n // OPS][0]
                            look_up(nc, act, un, u, u % P_RING, u % Q_RING, 16 * (u // Q_RING + 1), u % 2 == 0, (n % OPS,))
                        if last_one and o == 0:
                            keep_hi(nc, act, un, t, EARLY_UNITS, unit_dest(EARLY_UNITS)[0], unit_bank(EARLY_UNITS))
                    for g in range(len(X_FINISH)):
                        x_hi(b + 1, g)
                    for i in range(TB):
                        x_hi(b + 1, len(X_FINISH) + i)
                        act.wait_ge(s_neg, TB * b + i + 1)
                        nc.scalar.activation(probs[:, i, :], ps[:, 4 + i, 0:SEQ], ACT.Exp, bias=neg[:, i:i + 1],
                                             scale=exp_out[:, parity:parity + 1], accum_out=sums[:, i:i + 1]).then_inc(s_probs, 1)

                def turned_probs(b):
                    act.wait_ge(s_pt, b + 1)
                    nc.scalar.activation(probsT[:, 0, :, :].rearrange("p k t -> p (k t)"), ps[:, 4, :], ACT.Copy,
                                         scale=P_SCALE).then_inc(s_ptev, 1)

                for g in range(XG):
                    x_hi(0, g)
                for u in range(2):
                    keep_hi(nc, act, un, t, u, unit_dest(u)[0], unit_bank(u))
                act.wait_ge(s_bias, 1)
                batches(nc.scalar.Fori, step)
                x_hi(BATCH, XG)
                turned_probs(BATCH - 1)
                for g in range(XG + 1, Y_GROUPS):
                    x_hi(BATCH, g)

            @block.vector
            def _(dve):
                LINKS = 6 * TB + 2
                seen = [0]

                def link(b, op):
                    seen[0] += 1
                    op.then_inc(s_self, 1)
                    dve.wait_ge(s_self, LINKS * b + seen[0])

                ln_links = [0]

                def link_ln(op):
                    ln_links[0] += 1
                    op.then_inc(s_ln, 1)
                    dve.wait_ge(s_ln, ln_links[0])

                def normalise(b):
                    for i in range(TB):
                        dve.wait_ge(s_t, 2 * XG * (b - 1) + HALVES * (i + 1))
                        dve.wait_ge(s_dot, TB * b)
                        nt = TB * b + i
                        nc.vector.tensor_scalar(xn[:, i, :], y[:, bass.ds(nt, 1), :].rearrange("p o d -> p (o d)"),
                                                t.mv[:, bass.ds(nt, 1), 0], t.rstd[:, bass.ds(nt, 1)],
                                                ALU.subtract, ALU.mult).then_inc(s_xn, 1)

                def bias_dots(b, parity):
                    for i in range(TB):
                        if not isinstance(b, int) or b > 0:
                            dve.wait_ge(s_xn, TB * (b - 1) + i + 1)
                        wait(dve, s_dot, TB * b + i)
                        nc.vector.tensor_tensor_reduce(out=dump[:, :], in0=xn[:, i, :], in1=t.key_row[:, :], scale=1.0, scalar=0.0,
                                                       op0=ALU.mult, op1=ALU.add,
                                                       accum_out=dots[:, parity, i:i + 1]).then_inc(s_dot, 1)

                def x_lo(b, g):
                    hi, lo = x_group(b, g)[1]
                    dve.wait_ge(s_xhi, XG * b + g + 1)
                    nc.vector.tensor_tensor(lo, ps[:, g % 2, :].rearrange("p (k t) -> p k t", k=4), hi,
                                            ALU.subtract).then_inc(s_xlo, 1)

                def normalise_y(i):
                    if i >= 2:
                        dve.wait_ge(s_t, 2 * XG * BATCH + HALVES * (i - 1))
                    nc.vector.tensor_scalar(yn[:, i % 2, :], y[:, i, :], t.mv[:, i, 0:1], t.rstd[:, i:i + 1],
                                            ALU.subtract, ALU.mult).then_inc(s_xn, 1)

                def key_max(b):
                    dve.wait_ge(s_keys, 16 * b)
                    nc.vector.tensor_reduce(kmax[:, :], keys[:, :, :], axis=AX.XY, op=ALU.max,
                                            apply_absolute_value=True).then_inc(s_kmax, 1)

                def key_scales(b, parity):
                    seen[0] = 0
                    col = slice(parity, parity + 1)
                    wait(dve, s_kall, b)
                    link(b, nc.vector.tensor_scalar(kall[:, :], kall[:, :], TINY, None, ALU.max))
                    link(b, nc.vector.reciprocal(rk[:, :], kall[:, :]))
                    nc.vector.tensor_scalar(k_in[:, :], rk[:, :], K_BOUND, None, ALU.mult).then_inc(s_kin, 1)
                    nc.vector.tensor_scalar(score_out[:, col], kall[:, :], t.r_out[:, :], 1.0 / K_BOUND, ALU.mult, ALU.mult)
                    nc.vector.tensor_scalar(exp_out[:, col], kall[:, :], t.r_out[:, :], SCORE_SCALE / K_BOUND, ALU.mult, ALU.mult)
                    nc.vector.tensor_scalar(att_out[:, col], kall[:, :], 1.0 / (K_BOUND * P_SCALE), None, ALU.mult).then_inc(s_out, 1)

                def keys_lo(b, g):
                    i, h = g // HALVES, g % HALVES
                    dve.wait_ge(s_kev, XG * b + g + 1)
                    if g == XG - 1:
                        dve.wait_ge(s_klo, TB * (b + 1))
                    nc.vector.tensor_tensor(keysT[:, 1, 4 * h:4 * h + 4, i * P:(i + 1) * P],
                                            ps[:, g % 2, :].rearrange("p (k t) -> p k t", k=4),
                                            keysT[:, 0, 4 * h:4 * h + 4, i * P:(i + 1) * P], ALU.subtract).then_inc(s_ktlo, 1)

                def probs_lo(b):
                    dve.wait_ge(s_ptev, b + 1)
                    nc.vector.scalar_tensor_tensor(out=probsT[:, 1, :, :].rearrange("p k t -> p (k t)"), in0=ps[:, 4, :], scalar=P_SCALE,
                                                   in1=probsT[:, 0, :, :].rearrange("p k t -> p (k t)"),
                                                   op0=ALU.mult, op1=ALU.subtract).then_inc(s_ptlo, 1)

                def softmax(b, parity):
                    dve.wait_ge(s_dot, TB * (b + 1))
                    dve.wait_ge(s_out, b + 1)
                    wait(dve, s_y, ATT * b)
                    for i in range(TB):
                        x_lo(b + 1, len(X_FINISH) + i)
                        dve.wait_ge(s_scores, TB * b + i + 1)
                        link(b, nc.vector.reduce_max(mx[:, i:i + 1], ps[:, 4 + i, 0:SEQ], AX.X))
                        link(b, nc.vector.scalar_tensor_tensor(out=row[:, i:i + 1], in0=dots[:, parity, i:i + 1], scalar=1.0 / X_SCALE,
                                                               in1=t.bias_dot[:, :], op0=ALU.mult, op1=ALU.add))
                        link(b, nc.vector.scalar_tensor_tensor(out=top[:, i:i + 1], in0=mx[:, i:i + 1], scalar=score_out[:, parity:parity + 1],
                                                               in1=row[:, i:i + 1], op0=ALU.mult, op1=ALU.add))
                        link(b, nc.vector.tensor_tensor(top[:, i:i + 1], row[:, i:i + 1], top[:, i:i + 1], ALU.subtract))
                        nc.vector.tensor_scalar(neg[:, i:i + 1], top[:, i:i + 1], SCORE_SCALE, None, ALU.mult).then_inc(s_neg, 1)
                    for i in range(TB):
                        dve.wait_ge(s_probs, TB * b + i + 1)
                        link(b, nc.vector.reciprocal(rsum[:, parity, i:i + 1], sums[:, i:i + 1]))
                        link(b, nc.vector.tensor_scalar(rsum[:, parity, i:i + 1], rsum[:, parity, i:i + 1],
                                                        att_out[:, parity:parity + 1], None, ALU.mult))

                def residual(b, parity):
                    for i in range(TB):
                        for h in range(HALVES):
                            n = i * HALVES + h
                            tile = y[:, bass.ds(TB * b + i, 1), h * BANK:(h + 1) * BANK].rearrange("p o d -> p (o d)")
                            dve.wait_ge(s_att, ATT * b + n + 1)
                            nc.vector.scalar_tensor_tensor(out=tile, in0=ps[:, 6 + n % 2, :], scalar=rsum[:, parity, i:i + 1],
                                                           in1=tile, op0=ALU.mult, op1=ALU.add).then_inc(s_y, 1)
                            if n in X_FINISH:
                                x_lo(b + 2, X_FINISH.index(n))

                def scales_of_most():
                    dve.wait_ge(s_stats, BATCH - 2)
                    most = slice(0, TB * (BATCH - 2))
                    for i in range(TB * (BATCH - 2)):
                        last = nc.vector.bn_aggr(t.mv[:, i, :], t.all_stats[:, i, :, :].rearrange("p a b -> p (a b)"))
                    link_ln(last)
                    for _ in rsqrt(nc, t.rstd[:, most], t.mv[:, most, 1], t.guess[:, most], t.var[:, most], link_ln):
                        pass

                def statistics(b):
                    for i in range(TB):
                        for h in range(HALVES):
                            tile = y[:, bass.ds(TB * b + i, 1), h * BANK:(h + 1) * BANK].rearrange("p o d -> p (o d)")
                            last = nc.vector.bn_stats(stats[:, i, h, :], tile)
                    last.then_inc(s_bn, 1)
                    dve.wait_ge(s_bn, b + 1)
                    nc.vector.tensor_copy(t.all_stats[:, bass.ds(TB * b, TB), :, :], stats[:, :, :, :]).then_inc(s_stats, 1)

                def step(b, parity):
                    first = isinstance(b, int) and b == 0
                    last_one = isinstance(b, int) and b == BATCH - 1
                    key_scales(b, parity)
                    if first:
                        for u in range(2, EARLY_UNITS):
                            keep_lo(nc, dve, un, t, u, *unit_dest(u), unit_bank(u))
                    else:
                        probs_lo(b - 1)
                    if last_one:
                        keep_lo(nc, dve, un, t, EARLY_UNITS, *unit_dest(EARLY_UNITS), unit_bank(EARLY_UNITS))
                        scales_of_most()
                        normalise_y(0)
                        normalise_y(1)
                    elif not first:
                        normalise(b + 1)
                        bias_dots(b + 1, 1 - parity)
                    units = LATER.get(b, ()) if isinstance(b, int) else ()
                    todo = (0 for u, _, _ in units for _ in factors(nc, dve, un, u, u % P_RING, u % 2 == 0))
                    for g in range(XG):
                        if units:
                            for _, _ in zip(range(FACTORS_AT[b][g]), todo):
                                pass
                        keys_lo(b, g)
                        if first and g == 0:
                            dve.wait_ge(s_bias, 1)
                            bias_dots(0, 0)
                        if first and g == 1:
                            normalise(1)
                    for _ in todo:
                        pass
                    if first:
                        for g in range(len(X_FINISH)):
                            x_lo(b + 1, g)
                    else:
                        residual(b - 1, 1 - parity)
                    if last_one:
                        normalise_y(2)
                    softmax(b, parity)
                    if first:
                        bias_dots(1, 1)
                    if not last_one:
                        key_max(b + 1)
                    if not first and not last_one:
                        statistics(b - 1)

                for g in range(XG):
                    x_lo(0, g)
                nc.vector.tensor_scalar(t.query_col[:, :], ps[:, COL_BANK, 0:KT], t.r_in[:, :], None, ALU.mult)
                nc.vector.tensor_copy(t.bias_dot[:, :], ps[:, COL_BANK, KT:KT + 1])
                nc.vector.tensor_copy(t.key_row[:, :].rearrange("p (h n) -> p h n", h=HALVES),
                                      ps[:, ROW_BANK:ROW_BANK + HALVES, :]).then_inc(s_bias, 1)
                for u in range(2):
                    keep_lo(nc, dve, un, t, u, *unit_dest(u), unit_bank(u))
                batches(nc.vector.Fori, step)
                x_lo(BATCH, XG)
                probs_lo(BATCH - 1)
                normalise_y(3)
                x_lo(BATCH, XG + 1)
                halves = iter([(i, half) for i in range(NT - 2 * TB, NT - TB) for half in range(HALVES)])

                def some_statistics(count):
                    for _, (i, half) in zip(range(count), halves):
                        nc.vector.bn_stats(t.all_stats[:, i, half, :], y[:, i, half * BANK:(half + 1) * BANK])

                some_statistics(2)
                for n in range(ATT):
                    i, h = n // HALVES, n % HALVES
                    cols = slice(h * BANK, (h + 1) * BANK)
                    dve.wait_ge(s_att, ATT * (BATCH - 1) + n + 1)
                    nc.vector.scalar_tensor_tensor(out=y[:, NT - TB + i, cols], in0=ps[:, 6 + n % 2, :], scalar=rsum[:, 1, i:i + 1],
                                                   in1=y[:, NT - TB + i, cols], op0=ALU.mult, op1=ALU.add).then_inc(s_y, 1)
                    if XG + Y_BETWEEN + n < Y_GROUPS:
                        x_lo(BATCH, XG + Y_BETWEEN + n)
                    if 0 < n < ATT - 1:
                        some_statistics(1)


def feed_forward(nc, t, un):
    with ExitStack() as st:
        def sb(name, shape, dt):
            return st.enter_context(nc.sbuf_tensor(name, shape, dt))

        def sem(name):
            return st.enter_context(nc.semaphore(name + "_f"))

        y, ps = t.y, t.ps
        wd = sb("wd", [P, 3, 2, DIM], F16)
        h = sb("h", [P, 3, 2, TOK], F16)
        act_buf = sb("act_buf", [P, 2, BANK], F32)
        gate_now = sb("gate_now", [P, 2], F32)
        xn = h[:, 2, :, :].rearrange("p a b -> p (a b)").bitcast(F32).rearrange("p (i d) -> p i d", i=2)
        names = ("s_xn", "s_xt", "s_xhi", "s_xlo", "s_g", "s_u", "s_silu", "s_h", "s_hhi", "s_hlo", "s_down", "s_y", "s_out", "s_gate",
                 "s_self")
        s_xn, s_xt, s_xhi, s_xlo, s_g, s_u, s_silu, s_h, s_hhi, s_hlo, s_down, s_y, s_out, s_gate, s_self = (
            sem(n) for n in names)
        HALVES = DIM // BANK
        OUT = NT * HALVES
        STORES = (4, 4, 4, 2, 1, 1)
        LATE_STEPS = 2
        XG = HALVES * NT // NBLK

        def weights_of(chunk_odd, down_parity, kind):
            mat, half = kind
            if mat < 2:
                return gate_up_dest(un, chunk_odd, mat, half)
            return [wd[:, slot_of(chunk_odd, down_parity), part, half * BANK:(half + 1) * BANK] for part in range(2)]

        def dest(p_parity, e):
            if e < 4:
                return weights_of(1, 0, (e // 2, e % 2))
            if e < 6:
                return weights_of(0, p_parity, (2, e - 4))
            if e < 10:
                return weights_of(0, 0, ((e - 6) // 2, e % 2))
            return weights_of(1, 0, (2, e - 10))

        def ahead(p, e, lead=LEAD):
            return (p, e + lead) if e + lead < EVENTS else (p + 1, e + lead - EVENTS)

        def exists(p, e):
            if isinstance(p, int) and p >= PERIODS:
                return False
            return has_unit(p, e)

        def count(p, e):
            u = FIRST_UNITS + EVENTS * p + e
            return u - 4 if isinstance(p, int) and p == PERIODS - 1 and e >= 10 else u

        def periods(eng_loop, period):
            period(0, 0)
            with eng_loop(0, (PERIODS - 2) // 2) as j:
                period(2 * j + 1, 1)
                period(2 * j + 2, 0)
            period(PERIODS - 1, (PERIODS - 1) % 2)

        def slot_number(u, e):
            return u if isinstance(u, int) else FIRST_UNITS + e

        def x_part(n, part):
            i, half = n // HALVES, n % HALVES
            i, n = i % (BANK // P), i // (BANK // P)
            return t.xT[:, n, part, 4 * half:4 * half + 4, i * P:(i + 1) * P]

        def next_x(p, e):
            return range((e + 1) * XG, (e + 2) * XG) if isinstance(p, int) and p == 0 and e < NBLK - 1 else ()

        with nc.Block() as block:
            @block.sync
            def _(sp):
                def load(u, ring, pair, chunk, kind):
                    if kind != (2, 0):
                        sp.wait_ge(un.s_act, OPS * (u + pair - Q_RING + 1))
                    load_unit(nc, sp, un, t, u, ring, chunk, kind)

                def period(p, parity):
                    for e in range(EVENTS):
                        if exists(p, e) and (e >= LEAD or not (isinstance(p, int) and p == 0)):
                            _, chunk, kind = unit_of(p, e)
                            u = count(p, e)
                            if not exists(p, e - 1) and kind == (2, 0):
                                sp.wait_ge(un.s_act, OPS * (u - Q_RING + 1))
                            load(u, slot_number(u, e) % Q_RING, e in (3, 9), chunk, kind)

                periods(nc.sync.Fori, period)
                start = 0
                for tiles in STORES:
                    sp.wait_ge(s_y, OUT * (PERIODS - 1) + (start + tiles) * HALVES)
                    sp.dma_start(t.out_t[:, start:start + tiles, :], y[:, start:start + tiles, :]).then_inc(s_out, 16)
                    start += tiles
                sp.wait_ge(s_out, 16 * len(STORES))

            @block.gpsimd
            def _(pool):
                def scale(p, e):
                    if exists(p, e):
                        _, chunk, kind = unit_of(p, e)
                        u = count(p, e)
                        scale_unit(nc, pool, un, t, u, slot_number(u, e) % P_RING, chunk, kind)

                def hidden_lo(p, parity, e):
                    odd, n = block_of(p, e)
                    b = NBLK * (2 * p + odd) + n
                    pool.wait_ge(s_hhi, b + 1)
                    cols = slice(n * BANK, (n + 1) * BANK)
                    s = slot_of(odd, parity)
                    nc.gpsimd.tensor_tensor(h[:, s, 1, cols], act_buf[:, n % 2, :], h[:, s, 0, cols], ALU.subtract).then_inc(s_hlo, 1)

                def period(p, parity):
                    for e in range(EVENTS):
                        scale(*ahead(p, e, LEAD + 1))
                        if block_of(p, e):
                            hidden_lo(p, parity, e)

                scale(0, LEAD)
                periods(nc.gpsimd.Fori, period)

            @block.scalar
            def _(act):
                def x_hi(n):
                    act.wait_ge(s_xt, n - XG + 1)
                    nc.scalar.copy(x_part(n, 0), ps[:, 6 + n % 2, :].rearrange("p (k t) -> p k t", k=4)).then_inc(s_xhi, 1)

                def unit_args(p, e):
                    u = count(p, e)
                    k = slot_number(u, e)
                    q_count = 16 * (k // Q_RING + 1)
                    if not isinstance(u, int):
                        q_count = q_count + 16 * (EVENTS // Q_RING) * p
                    return u, k % P_RING, k % Q_RING, q_count, e % 2 == 0

                def weights_hi(p, parity, e):
                    keep_hi(nc, act, un, t, count(p, e), dest(parity, e)[0], e % 2)

                def silu(p, e):
                    odd, n = block_of(p, e)
                    b = NBLK * (2 * p + odd) + n
                    act.wait_ge(s_g, b + 1)
                    wait(act, s_hlo, b - 1)
                    if e == 0:
                        act.wait_ge(s_gate, p + 1)
                    nc.scalar.activation(act_buf[:, n % 2, :], ps[:, 2 + n % 2, :], ACT.Silu,
                                         scale=gate_now[:, odd:odd + 1]).then_inc(s_silu, 1)

                def hidden_hi(p, parity, e):
                    odd, n = block_of(p, e)
                    act.wait_ge(s_h, NBLK * (2 * p + odd) + n + 1)
                    nc.scalar.copy(h[:, slot_of(odd, parity), 0, n * BANK:(n + 1) * BANK], act_buf[:, n % 2, :]).then_inc(s_hhi, 1)

                def period(p, parity):
                    for e in range(EVENTS):
                        p2, e2 = ahead(p, e)
                        args = unit_args(p2, e2) if exists(p2, e2) else None
                        groups = next_x(p, e)
                        if exists(p, e):
                            weights_hi(p, parity, e)
                        for i in range(OPS):
                            if i == OPS // 2 and block_of(p, e):
                                silu(p, e)
                            if args and i > 0:
                                look_up(nc, act, un, *args, (i,))
                            if groups:
                                x_hi(groups[i])
                        if exists(*ahead(p, e, LEAD + 1)):
                            look_up(nc, act, un, *unit_args(*ahead(p, e, LEAD + 1)), (0,))
                        if block_of(p, e):
                            hidden_hi(p, parity, e)

                look_up(nc, act, un, *unit_args(0, LEAD), (0,))
                periods(nc.scalar.Fori, period)

            @block.vector
            def _(dve):
                def norm(i):
                    wait(dve, s_xt, HALVES * (i - 1) - XG)
                    nc.vector.tensor_scalar(xn[:, i % 2, :], y[:, i, :], t.mv[:, i, 0:1], t.rstd[:, i:i + 1],
                                            ALU.subtract, ALU.mult).then_inc(s_xn, 1)

                def x_lo(n):
                    dve.wait_ge(s_xhi, n - XG + 1)
                    nc.vector.tensor_tensor(x_part(n, 1), ps[:, 6 + n % 2, :].rearrange("p (k t) -> p k t", k=4),
                                            x_part(n, 0), ALU.subtract).then_inc(s_xlo, 1)

                def weights_lo(p, parity, e):
                    keep_lo(nc, dve, un, t, count(p, e), *dest(parity, e), e % 2)

                def hidden(p, e):
                    odd, n = block_of(p, e)
                    b = NBLK * (2 * p + odd) + n
                    dve.wait_ge(s_u, b + 1)
                    dve.wait_ge(s_silu, b + 1)
                    nc.vector.scalar_tensor_tensor(out=act_buf[:, n % 2, :], in0=ps[:, 4 + n % 2, :],
                                                   scalar=t.up_out[:, bass.ds(2 * p + odd, 1)], in1=act_buf[:, n % 2, :],
                                                   op0=ALU.mult, op1=ALU.mult).then_inc(s_h, 1)

                def add_down(p, n):
                    i, hh = n // HALVES, n % HALVES
                    cols = slice(hh * BANK, (hh + 1) * BANK)
                    dve.wait_ge(s_down, OUT * p + n + 1)
                    nc.vector.scalar_tensor_tensor(out=y[:, i, cols], in0=ps[:, 6 + n % 2, :], scalar=t.y_out[:, 0:1],
                                                   in1=y[:, i, cols], op0=ALU.mult, op1=ALU.add).then_inc(s_y, 1)

                def period(p, parity):
                    wait(dve, s_silu, 2 * NBLK * p)
                    nc.vector.tensor_copy(gate_now[:, :], t.gate_out[:, bass.ds(2 * p, 2)]).then_inc(s_gate, 1)
                    for e in range(EVENTS):
                        if exists(p, e):
                            weights_lo(p, parity, e)
                        p2, e2 = ahead(p, e)
                        todo = iter(())
                        if exists(p2, e2):
                            u = count(p2, e2)
                            todo = factors(nc, dve, un, u, slot_number(u, e2) % P_RING, e2 % 2 == 0)
                        for n in next_x(p, e):
                            if n % HALVES == 0 and n // HALVES + 1 < NT:
                                if n // HALVES + 1 == NT - 2 * TB:
                                    for _ in late:
                                        pass
                                norm(n // HALVES + 1)
                            x_lo(n)
                            next(todo, None)
                            for _, _ in zip(range(LATE_STEPS), late):
                                pass
                        if down_of(p, e) is not None:
                            for n in range(OUT // 4):
                                add_down(p - 1, down_of(p, e) * OUT // 4 + n)
                                next(todo, None)
                        for _ in todo:
                            pass
                        if block_of(p, e):
                            hidden(p, e)

                seen = [0]

                def link(op):
                    seen[0] += 1
                    op.then_inc(s_self, 1)
                    dve.wait_ge(s_self, seen[0])

                def last_statistics():
                    for i in range(NT - TB, NT):
                        for half in range(HALVES):
                            last = nc.vector.bn_stats(t.all_stats[:, i, half, :], y[:, i, half * BANK:(half + 1) * BANK])
                            yield
                    link(last)
                    rest = slice(NT - 2 * TB, NT)
                    for i in range(NT - 2 * TB, NT):
                        last = nc.vector.bn_aggr(t.mv[:, i, :], t.all_stats[:, i, :, :].rearrange("p a b -> p (a b)"))
                    link(last)
                    yield from rsqrt(nc, t.rstd[:, rest], t.mv[:, rest, 1], t.guess[:, rest], t.var[:, rest], link)

                late = last_statistics()
                norm(NT // NBLK)
                periods(nc.vector.Fori, period)
                for n in range(OUT):
                    add_down(PERIODS - 1, n)

            @block.tensor
            def _(pe):
                def turn(u, slot, bank):
                    pe.wait_ge(un.s_wlo, u - 1)
                    turn_unit(nc, pe, un, t, u, slot, bank)

                def turn_x(n):
                    pe.wait_ge(s_xn, (n - XG) // HALVES + 1)
                    wait(pe, s_xlo, n - XG - 1)
                    for k in range(4):
                        src = xn[:, n // HALVES % 2, (n % HALVES * 4 + k) * P:(n % HALVES * 4 + k + 1) * P]
                        last = nc.tensor.transpose(ps[:, 6 + n % 2, k * P:(k + 1) * P], src, t.ident[:, :])
                    last.then_inc(s_xt, 1)

                def gate_up(p, e):
                    odd, n = block_of(p, e)
                    b = NBLK * (2 * p + odd) + n
                    wait(pe, s_h, b - 1)
                    groups = iter(next_x(p, e))
                    for mat, done in ((0, s_g), (1, s_u)):
                        for k in range(KT):
                            for j, (a, c) in enumerate(PARTS):
                                last = nc.tensor.matmul(ps[:, 2 + 2 * mat + n % 2, :], un.wgu[:, odd, mat, a, k, :],
                                                        t.xT[:, n, c, k, :],
                                                        start=k == 0 and j == 0, stop=k == KT - 1 and j == 2)
                            if k % 2:
                                for group in groups:
                                    turn_x(group)
                                    break
                        last.then_inc(done, 1)

                def down(p, parity, n):
                    i, hh = n // HALVES, n % HALVES
                    if n >= 2:
                        pe.wait_ge(s_y, OUT * p + n - 1)
                    todo = [(s, a, c) for s in (slot_of(0, parity), slot_of(1, parity)) for a, c in PARTS]
                    for m, (s, a, c) in enumerate(todo):
                        last = nc.tensor.matmul(ps[:, 6 + n % 2, :], h[:, s, a, i * P:(i + 1) * P],
                                                wd[:, s, c, hh * BANK:(hh + 1) * BANK], start=m == 0, stop=m == len(todo) - 1)
                    last.then_inc(s_down, 1)

                def down_ready(p):
                    pe.wait_ge(s_hlo, NBLK * (2 * p + 2))
                    pe.wait_ge(un.s_wlo, count(p, EVENTS - 1) + 1)

                def period(p, parity):
                    for e in range(EVENTS):
                        if exists(p, e):
                            u = count(p, e)
                            turn(u, slot_number(u, e) % P_RING, e % 2)
                        if e == 0:
                            pe.wait_ge(un.s_wlo, FIRST_UNITS + EVENTS * (p - 1) + 10 if not isinstance(p, int) or p else FIRST_UNITS)
                        if block_of(p, e) == (1, 0):
                            pe.wait_ge(un.s_wlo, FIRST_UNITS + EVENTS * p + 4)
                        if 0 < e < NBLK and isinstance(p, int) and p == 0:
                            pe.wait_ge(s_xlo, e * XG)
                        if block_of(p, e):
                            gate_up(p, e)
                        if down_of(p, e) is not None:
                            if e == 4:
                                down_ready(p - 1)
                            for n in range(OUT // 4):
                                down(p - 1, 1 - parity, down_of(p, e) * OUT // 4 + n)

                periods(nc.tensor.Fori, period)
                last_pair = PERIODS - 1
                down_ready(last_pair)
                for n in range(OUT):
                    down(last_pair, last_pair % 2, n)


_INS = ["x", "ctx_4096", "L0_xattn_Wq", "L0_xattn_bq", "L0_xattn_Wk", "L0_xattn_bk", "L0_ffn_gate_q",
        "L0_ffn_gate_absmax", "L0_ffn_up_q", "L0_ffn_up_absmax", "L0_ffn_down_q", "L0_ffn_down_absmax"]


def kernel(**inputs):
    import concourse.bacc as bacc
    from concourse.bass_utils import run_bass_kernel_spmd

    nc = bacc.Bacc("TRN2", target_bir_lowering=False, num_devices=1)
    arrays, args = {}, []
    for name in _INS:
        a = np.ascontiguousarray(inputs[name])
        arrays[f"in_{name}"] = a
        args.append(nc.dram_tensor(f"in_{name}", a.shape, mybir.dt.from_np(a.dtype), kind="ExternalInput").ap())
    args.append(nc.dram_tensor("out_0", (BATCH, SEQ, DIM), F32, kind="ExternalOutput").ap())
    xattn_ffn_kernel(nc, *args)
    r = run_bass_kernel_spmd(nc, [arrays], core_ids=[0])
    return r.results[0]["out_0"]
```
